# Optimizing a Trainium2 kernel written in Bass

```python
import numpy as np
import jax
import jax.numpy as jnp

def _softmax(x, axis=-1):
    return jax.nn.softmax(x, axis=axis)

def _gelu(x):
    return jax.nn.gelu(x, approximate=True)

def _silu(x):
    return jax.nn.silu(x)

def _sigmoid(x):
    return jax.nn.sigmoid(x)

def _layernorm(x, axis=-1, eps=1e-05):
    m = jnp.mean(x, axis=axis, keepdims=True)
    v = jnp.var(x, axis=axis, keepdims=True)
    return (x - m) / jnp.sqrt(v + eps)

def _scatter_add(tgt, idx, src, axis=0):
    return tgt.at[idx].add(src)

def _segment_sum(src, seg, n):
    return jax.ops.segment_sum(src, seg, n)
kernel_name = 'mk_adaln_ffn_d1_seqx_r4_7a4c13'

def setup_inputs(seed: int=0):
    np.random.seed(seed)
    _w = jnp.asarray

    def _rec_inputs():
        import jax
        import jax.numpy as jnp
        _rk = jax.random.key(seed)
        x = 7.22e-05 + 1 * jax.random.normal(jax.random.fold_in(_rk, 1), (32, 256, 256), jnp.float32)
        _lenS = 256 - jax.random.randint(jax.random.fold_in(_rk, 7), (32,), 0, max(1, 256 // 4) + 1, jnp.int32)
        _lenS2 = 256 - jax.random.randint(jax.random.fold_in(_rk, 8), (32,), 0, max(1, 256 // 4) + 1, jnp.int32)
        fside_BxSxS_0 = 4.13588e-05 + 0.999923 * jax.random.normal(jax.random.fold_in(_rk, 11), (32, 256, 256), jnp.float32)
        itok_B_0_5 = jax.random.randint(jax.random.fold_in(_rk, 12), (32,), 0, 6, jnp.int32)
        return (x, fside_BxSxS_0, itok_B_0_5)
    x, fside_BxSxS_0, itok_B_0_5 = _rec_inputs()

    def _L0_cond_setup():
        import jax, jax.numpy as jnp
        import numpy as np
        B, S, D = (8, 256, 256)
        NUM_STAGES = 6
        key = jax.random.key(seed)
        k1, k2, k3, k4, k5 = jax.random.split(key, 5)
        return {'query': jax.random.normal(k1, (B, S, D), dtype=jnp.float32), 'key': jax.random.normal(k2, (B, S, D), dtype=jnp.float32), 'value': jax.random.normal(k3, (B, S, D), dtype=jnp.float32), 'braak_embed': jax.random.normal(k4, (NUM_STAGES, D), dtype=jnp.float32), 'braak_stages': jax.random.randint(k5, (B,), 0, NUM_STAGES, dtype=jnp.int64)}
    _L0_cond_all = _L0_cond_setup()
    _L0_cond_in = {k: v for k, v in _L0_cond_all.items() if k in ('braak_embed',)}
    del _L0_cond_all

    def _L0_ffn_setup():
        import jax, jax.numpy as jnp
        import numpy as np
        B, S, D, F, E, R, K = (1, 128, 256, 1024, 8, 16, 2)
        SCALING = 32.0 / 16.0
        EPS = 1e-06

        def _forward(x, norm_w, w1, w3, w2, gate_w, a1, b1, a3, b3, a2, b2):
            Bq, Sq, Dq = x.shape
            nx = x * jax.lax.rsqrt(jnp.mean(x * x, axis=-1, keepdims=True) + EPS) * norm_w
            t = nx.reshape(-1, Dq)
            probs = jax.nn.softmax(t @ gate_w.T, axis=-1)
            topw, topi = jax.lax.top_k(probs, K)
            topw = topw / jnp.sum(topw, axis=-1, keepdims=True)
            weights = jnp.sum(jax.nn.one_hot(topi, E, dtype=t.dtype) * topw[..., None], axis=1)
            base1 = t @ w1.T
            base3 = t @ w3.T
            h1 = base1[None] + SCALING * jnp.einsum('etr,efr->etf', jnp.einsum('td,erd->etr', t, a1), b1)
            h3 = base3[None] + SCALING * jnp.einsum('etr,efr->etf', jnp.einsum('td,erd->etr', t, a3), b3)
            act = jax.nn.silu(h1) * h3
            out_e = jnp.einsum('etf,df->etd', act, w2) + SCALING * jnp.einsum('etr,edr->etd', jnp.einsum('etf,erf->etr', act, a2), b2)
            out = jnp.einsum('te,etd->td', weights, out_e)
            return out.reshape(Bq, Sq, Dq)
        key = jax.random.key(seed)
        ks = jax.random.split(key, 12)
        w = lambda k, shape: jax.random.normal(k, shape, dtype=jnp.float32) * 0.02
        return {'x': jax.random.normal(ks[0], (B, S, D), dtype=jnp.float32), 'norm_w': jnp.ones((D,), jnp.float32), 'w1': w(ks[1], (F, D)), 'w3': w(ks[2], (F, D)), 'w2': w(ks[3], (D, F)), 'gate_w': w(ks[4], (E, D)), 'a1': w(ks[5], (E, R, D)), 'b1': w(ks[6], (E, F, R)), 'a3': w(ks[7], (E, R, D)), 'b3': w(ks[8], (E, F, R)), 'a2': w(ks[9], (E, R, F)), 'b2': w(ks[10], (E, D, R))}
    _L0_ffn_all = _L0_ffn_setup()
    _L0_ffn_in = {k: v for k, v in _L0_ffn_all.items() if k in ('norm_w', 'w1', 'w3', 'w2', 'gate_w', 'a1', 'b1', 'a3', 'b3', 'a2', 'b2')}
    del _L0_ffn_all
    return {'x': x, 'fside_BxSxS_0': fside_BxSxS_0, 'itok_B_0_5': itok_B_0_5, 'L0_cond_braak_embed': _L0_cond_in['braak_embed'], 'L0_ffn_norm_w': _L0_ffn_in['norm_w'], 'L0_ffn_w1': _L0_ffn_in['w1'], 'L0_ffn_w3': _L0_ffn_in['w3'], 'L0_ffn_w2': _L0_ffn_in['w2'], 'L0_ffn_gate_w': _L0_ffn_in['gate_w'], 'L0_ffn_a1': _L0_ffn_in['a1'], 'L0_ffn_b1': _L0_ffn_in['b1'], 'L0_ffn_a3': _L0_ffn_in['a3'], 'L0_ffn_b3': _L0_ffn_in['b3'], 'L0_ffn_a2': _L0_ffn_in['a2'], 'L0_ffn_b2': _L0_ffn_in['b2']}

def reference(x, fside_BxSxS_0, itok_B_0_5, L0_cond_braak_embed, L0_ffn_norm_w, L0_ffn_w1, L0_ffn_w3, L0_ffn_w2, L0_ffn_gate_w, L0_ffn_a1, L0_ffn_b1, L0_ffn_a3, L0_ffn_b3, L0_ffn_a2, L0_ffn_b2):
    import jax
    import jax.numpy as jnp

    def _L0_cond_ref(query, key, value, braak_embed, braak_stages):
        import jax, jax.numpy as jnp
        import numpy as np
        B, S, D = (8, 256, 256)
        NUM_STAGES = 6
        bias = braak_embed[braak_stages][..., None]
        q = query + bias
        attn = jnp.einsum('bsd,btd->bst', q, key)
        attn = jax.nn.softmax(attn, axis=-1)
        return jnp.einsum('bst,btd->bsd', attn, value)

    def _L0_ffn_ref(x, norm_w, w1, w3, w2, gate_w, a1, b1, a3, b3, a2, b2):
        import jax, jax.numpy as jnp
        import numpy as np
        B, S, D, F, E, R, K = (1, 128, 256, 1024, 8, 16, 2)
        SCALING = 32.0 / 16.0
        EPS = 1e-06

        def _forward(x, norm_w, w1, w3, w2, gate_w, a1, b1, a3, b3, a2, b2):
            Bq, Sq, Dq = x.shape
            nx = x * jax.lax.rsqrt(jnp.mean(x * x, axis=-1, keepdims=True) + EPS) * norm_w
            t = nx.reshape(-1, Dq)
            probs = jax.nn.softmax(t @ gate_w.T, axis=-1)
            topw, topi = jax.lax.top_k(probs, K)
            topw = topw / jnp.sum(topw, axis=-1, keepdims=True)
            weights = jnp.sum(jax.nn.one_hot(topi, E, dtype=t.dtype) * topw[..., None], axis=1)
            base1 = t @ w1.T
            base3 = t @ w3.T
            h1 = base1[None] + SCALING * jnp.einsum('etr,efr->etf', jnp.einsum('td,erd->etr', t, a1), b1)
            h3 = base3[None] + SCALING * jnp.einsum('etr,efr->etf', jnp.einsum('td,erd->etr', t, a3), b3)
            act = jax.nn.silu(h1) * h3
            out_e = jnp.einsum('etf,df->etd', act, w2) + SCALING * jnp.einsum('etr,edr->etd', jnp.einsum('etf,erf->etr', act, a2), b2)
            out = jnp.einsum('te,etd->td', weights, out_e)
            return out.reshape(Bq, Sq, Dq)
        return _forward(x, norm_w, w1, w3, w2, gate_w, a1, b1, a3, b3, a2, b2)
    x = x + _L0_ffn_ref(_L0_cond_ref(x, fside_BxSxS_0, fside_BxSxS_0, L0_cond_braak_embed, itok_B_0_5), L0_ffn_norm_w, L0_ffn_w1, L0_ffn_w3, L0_ffn_w2, L0_ffn_gate_w, L0_ffn_a1, L0_ffn_b1, L0_ffn_a3, L0_ffn_b3, L0_ffn_a2, L0_ffn_b2)
    return x

_drawn_inputs = setup_inputs


def setup_inputs(seed=0):
    import zlib

    import numpy as np

    out = dict(_drawn_inputs(seed))
    spreads = {'L0_ffn_norm_w': (1.0, 0.6)}
    factors = {'L0_ffn_gate_w': 8.0,
     'L0_ffn_a1': 8.0,
     'L0_ffn_b1': 8.0,
     'L0_ffn_a3': 8.0,
     'L0_ffn_b3': 8.0,
     'L0_ffn_a2': 8.0,
     'L0_ffn_b2': 8.0}
    for name, (base, spread) in spreads.items():
        noise = np.random.default_rng([zlib.crc32(name.encode()), seed]).standard_normal(out[name].shape)
        drawn = base * np.exp(spread * noise) if base else spread * noise
        out[name] = jnp.asarray(drawn.astype(out[name].dtype))
    for name, factor in factors.items():
        out[name] = (out[name] * factor).astype(out[name].dtype)
    return out
```

```python
from contextlib import ExitStack

import concourse.bass as bass
from concourse import mybir
from concourse.alu_op_type import AluOpType as ALU

F32 = mybir.dt.float32
F32R = mybir.dt.float32r
BF16 = mybir.dt.bfloat16
I32 = mybir.dt.int32
ACT = mybir.ActivationFunctionType
AXIS = mybir.AxisListType

P = 128
BATCH, S, D = 32, 256, 256
F, E, R = 1024, 8, 16
STAGES = 6
ER = E * R
SC = S // P
DC = D // P
FC = F // P
TILE = 512
KT = TILE // P
TILES = BATCH * S // TILE
COLS = BATCH * SC
SCALING = 32.0 / 16.0
EPS = 1e-06
RING = 4
ROUTE = 2 * E + 3
DM0, RHO, RSTD, W1ST = E, 2 * E, 2 * E + 1, 2 * E + 2


def adaln_moe_ffn(nc, x, side, itok, embed, norm_w, w1, w3, w2, gate_w, a1, b1, a3, b3, a2, b2, out):
    ctx = ExitStack()
    with ctx:
        def sem(name):
            return ctx.enter_context(nc.semaphore(name))

        def sems(name, n):
            return [sem(f"{name}{k}") for k in range(n)]

        def sb(stack, name, shape, dt=F32):
            return stack.enter_context(nc.sbuf_tensor(name, shape, dt))

        bank = [ctx.enter_context(nc.psum_tensor(f"bank{k}", [P, 512], F32)) for k in range(8)]
        t_scratch = nc.dram_tensor("t_scratch", [BATCH * P, DC * S], F32, kind="Internal").ap()

        ident = sb(ctx, "ident", [P, P])
        ones = sb(ctx, "ones", [P, 1])
        rank_key = sb(ctx, "rank_key", [P, E])
        stage_id = sb(ctx, "stage_id", [STAGES, 1])

        def split(name, shape):
            return sb(ctx, name + "_hi", shape, F32R), sb(ctx, name + "_lo", shape, F32R)

        w1T = split("w1T", [P, DC, F])
        w3T = split("w3T", [P, DC, F])
        w2T = split("w2T", [P, FC, D])
        a2T = split("a2T", [P, FC, ER])
        a13T = split("a13T", [P, DC, 2, ER])
        b1T = split("b1T", [ER, F])
        b3T = split("b3T", [ER, F])
        b2T = split("b2T", [ER, D])
        gateT = sb(ctx, "gateT", [P, DC, E])
        logits = sb(ctx, "logits", [P, COLS, E])
        mean_sq = sb(ctx, "mean_sq", [P, COLS])
        route = sb(ctx, "route", [P, COLS, ROUTE])

        early = ExitStack()
        w1_in = sb(early, "w1_in", [P, FC, D])
        w3_in = sb(early, "w3_in", [P, FC, D])
        w2_in = sb(early, "w2_in", [P, DC, F])
        b1_in = sb(early, "b1_in", [P, E, FC * R])
        b3_in = sb(early, "b3_in", [P, E, FC * R])
        b1_by_j = sb(early, "b1_by_j", [P, FC, E, R])
        b3_by_j = sb(early, "b3_by_j", [P, FC, E, R])
        a1_in = sb(early, "a1_in", [ER, D])
        a3_in = sb(early, "a3_in", [ER, D])
        a2_in = sb(early, "a2_in", [ER, F])
        b2_in = sb(early, "b2_in", [P, DC, E, R])
        gate_in = sb(early, "gate_in", [E, D])
        nw = sb(early, "nw", [P, DC])
        embed_in = sb(early, "embed_in", [STAGES, S])
        itok_in = sb(early, "itok_in", [STAGES, BATCH], I32)
        itok_f = sb(early, "itok_f", [STAGES, BATCH])
        stage_hot = sb(early, "stage_hot", [STAGES, BATCH])
        bias = sb(early, "bias", [P, SC, BATCH])
        x_in = [sb(early, f"x_in{k}", [P, SC, D]) for k in range(RING)]
        kv = [sb(early, f"kv{k}", [P, SC, D]) for k in range(RING)]
        q = [sb(early, f"q{k}", [P, SC, D]) for k in range(2)]
        qT = [sb(early, f"qT{k}", [P, DC * S]) for k in range(2)]
        kT = [sb(early, f"kT{k}", [P, DC * S]) for k in range(2)]
        prob = [sb(early, f"prob{k}", [P, SC, S]) for k in range(2)]
        probT = [sb(early, f"probT{k}", [P, SC * S]) for k in range(2)]
        oT = [sb(early, f"oT{k}", [P, DC * S]) for k in range(2)]
        oT_sq = [sb(early, f"oT_sq{k}", [P, DC * S]) for k in range(2)]
        neg_max = [sb(early, f"neg_max{k}", [P, SC]) for k in range(2)]
        row_sum = [sb(early, f"row_sum{k}", [P, SC]) for k in range(RING)]
        eps_r2 = sb(early, "eps_r2", [P, SC])
        r_z = sb(early, "r_z", [P, COLS])
        r_y = sb(early, "r_y", [P, COLS])
        r_t = sb(early, "r_t", [P, COLS])
        top1 = sb(early, "top1", [P, COLS])
        top2 = sb(early, "top2", [P, COLS])
        r_key = sb(early, "r_key", [P, COLS])
        r_eq = sb(early, "r_eq", [P, COLS, E])
        r_rest = sb(early, "r_rest", [P, COLS, E])
        r_hot2 = sb(early, "r_hot2", [P, COLS, E])
        early.close()

        late = ctx
        t_in = [sb(late, f"t_in{k}", [P, 2, DC, S]) for k in range(2)]
        t_scaled = sb(late, "t_scaled", [P, DC, TILE])
        t_hi = [sb(late, f"t_hi{k}", [P, DC, TILE], F32R) for k in range(2)]
        t_lo = [sb(late, f"t_lo{k}", [P, DC, TILE], F32R) for k in range(2)]
        rt = [sb(late, f"rt{k}", [P, KT, 3]) for k in range(2)]
        hot_x = sb(late, "hot_x", [P, KT, E, R])
        hot_dx = sb(late, "hot_dx", [P, KT, E, R])
        mask1 = [sb(late, f"mask1_{k}", [ER, TILE], BF16) for k in range(2)]
        mask_d = [sb(late, f"mask_d{k}", [ER, TILE], BF16) for k in range(2)]
        rho = [sb(late, f"rho{k}", [P, TILE]) for k in range(2)]
        v_full = [sb(late, f"v_full{k}", [ER, TILE]) for k in range(2)]
        v_hi = [sb(late, f"v_hi{k}", [ER, TILE], F32R) for k in range(4)]
        v_lo = [sb(late, f"v_lo{k}", [ER, TILE], F32R) for k in range(4)]
        silu_a = [sb(late, f"silu_a{k}", [P, TILE]) for k in range(2)]
        silu_b = [sb(late, f"silu_b{k}", [P, TILE]) for k in range(2)]
        act_a = [sb(late, f"act_a{k}", [P, TILE]) for k in range(2)]
        act_b = sb(late, "act_b", [P, TILE])
        act_br = [sb(late, f"act_br{k}", [P, TILE]) for k in range(2)]
        act_s = [sb(late, f"act_s{k}", [P, TILE]) for k in range(2)]
        s_hi = [sb(late, f"s_hi{k}", [P, TILE], F32R) for k in range(2)]
        s_lo = [sb(late, f"s_lo{k}", [P, TILE], F32R) for k in range(2)]
        br_hi = [sb(late, f"br_hi{k}", [P, TILE], F32R) for k in range(2)]
        br_lo = [sb(late, f"br_lo{k}", [P, TILE], F32R) for k in range(2)]
        z_a = sb(late, "z_a", [ER, TILE])
        z_b = sb(late, "z_b", [ER, TILE])
        z_hi = sb(late, "z_hi", [ER, TILE], F32R)
        z_lo = sb(late, "z_lo", [ER, TILE], F32R)
        yT = sb(late, "yT", [P, DC, TILE])
        x_out = [sb(late, f"x_out{k}", [P, KT, D]) for k in range(2)]

        const_ready = sem("const_ready")
        w_loaded = sem("w_loaded")
        stage_ready = sem("stage_ready")
        b_ordered = sem("b_ordered")
        wT_ready = sem("wT_ready")
        w_hi_ready = sem("w_hi_ready")
        w_lo_ready = sem("w_lo_ready")
        bias_ready = sem("bias_ready")
        seq_loaded = sems("seq_loaded", RING)
        q_ready = sem("q_ready")
        qkT_ready = sem("qkT_ready")
        qT_copied = sem("qT_copied")
        kT_copied = sem("kT_copied")
        scores_ready = sem("scores_ready")
        max_ready = sem("max_ready")
        prob_ready = sem("prob_ready")
        probT_ready = sem("probT_ready")
        probT_copied = sem("probT_copied")
        o_ready = sem("o_ready")
        oT_copied = sem("oT_copied")
        oT_squared = sem("oT_squared")
        gate_ready = sem("gate_ready")
        eps_ready = sem("eps_ready")
        gate_read = sem("gate_read")
        t_stored = sems("t_stored", 2)
        route_step = sem("route_step")
        route_chain = sem("route_chain")
        route_act = sem("route_act")
        route_done = sem("route_done")

        t_loaded = sems("t_loaded", 2)
        x_loaded = sems("x_loaded", 2)
        out_stored = sems("out_stored", 2)
        rt_ready = sem("rt_ready")
        masks_ready = sem("masks_ready")
        mask1_copied = sem("mask1_copied")
        mask_d_copied = sem("mask_d_copied")
        scales_ready = sem("scales_ready")
        rho_copied = sem("rho_copied")
        t_scaled_ready = sem("t_scaled_ready")
        t_hi_ready = sem("t_hi_ready")
        t_lo_ready = sem("t_lo_ready")
        u_ready = sem("u_ready")
        v_ready = sem("v_ready")
        v_hi_ready = sem("v_hi_ready")
        v_lo_ready = sem("v_lo_ready")
        h1_first = sem("h1_first")
        h3_first = sem("h3_first")
        h1_second = sem("h1_second")
        h3_second = sem("h3_second")
        silu_a_ready = sem("silu_a_ready")
        silu_b_ready = sem("silu_b_ready")
        act_a_ready = sem("act_a_ready")
        act_b_ready = sem("act_b_ready")
        act_br_ready = sem("act_br_ready")
        act_s_ready = sem("act_s_ready")
        s_hi_ready = sem("s_hi_ready")
        br_hi_ready = sem("br_hi_ready")
        down_in_ready = sem("down_in_ready")
        down_done = sem("down_done")
        z_a_ready = sem("z_a_ready")
        z_b_ready = sem("z_b_ready")
        z_ready = sem("z_ready")
        z_hi_ready = sem("z_hi_ready")
        z_lo_ready = sem("z_lo_ready")
        y_ready = sem("y_ready")
        y0_copied = sem("y0_copied")
        y1_copied = sem("y1_copied")
        yT_ready = sem("yT_ready")
        out_ready = sem("out_ready")

        block = ctx.enter_context(nc.Block())

        def f32(ap):
            return ap.bitcast(F32)

        jobs = []

        def nw_at(c):
            return nw[:, c:c + 1]

        a13_in = (a1_in, a3_in)
        jobs.append(([(128 * (2 * c + w), 128, a13_in[w][:, c * P:(c + 1) * P], ER)
                      for c in range(DC) for w in range(2)],
                     [(256 * c, 256, a13T[0][:, c].rearrange("p w e -> p (w e)"),
                       a13T[1][:, c].rearrange("p w e -> p (w e)"), nw_at(c)) for c in range(DC)]))
        for src, dst in ((w1_in, w1T), (w3_in, w3T)):
            for c in range(DC):
                for j0 in range(0, FC, 4):
                    jobs.append(([(128 * k, 128, src[:, j0 + k, c * P:(c + 1) * P], P) for k in range(4)],
                                 [(0, 512, dst[0][:, c, j0 * P:(j0 + 4) * P],
                                   dst[1][:, c, j0 * P:(j0 + 4) * P], nw_at(c))]))
        for src, dst in ((b1_by_j, b1T), (b3_by_j, b3T)):
            for j0 in range(0, FC, 4):
                jobs.append(([(128 * k, 128, src[:, j0 + k].rearrange("p e r -> p (e r)"), P) for k in range(4)],
                             [(0, 512, dst[0][:, j0 * P:(j0 + 4) * P],
                               dst[1][:, j0 * P:(j0 + 4) * P], SCALING)]))
        for j0 in range(0, FC, 2):
            jobs.append(([(128 * (2 * k + c), 128, w2_in[:, c, j0 + k:F:FC], P)
                          for k in range(2) for c in range(DC)],
                         [(0, 512, w2T[0][:, j0:j0 + 2].rearrange("p j d -> p (j d)"),
                           w2T[1][:, j0:j0 + 2].rearrange("p j d -> p (j d)"), 1.0)]))
        for j0 in range(0, FC, 4):
            jobs.append(([(128 * k, 128, a2_in[:, j0 + k:F:FC], ER) for k in range(4)],
                         [(0, 512, a2T[0][:, j0:j0 + 4].rearrange("p j e -> p (j e)"),
                           a2T[1][:, j0:j0 + 4].rearrange("p j e -> p (j e)"), 1.0)]))
        jobs.append(([(128 * c, 128, b2_in[:, c].rearrange("p e r -> p (e r)"), P) for c in range(DC)]
                     + [(256 + E * c, E, gate_in[:, c * P:(c + 1) * P], E) for c in range(DC)],
                     [(0, 256, b2T[0][:, :], b2T[1][:, :], SCALING)]
                     + [(256 + E * c, E, gateT[:, c], None, nw_at(c)) for c in range(DC)]))
        JOBS = len(jobs)
        W_LOADS = 14

        qT_bank, kT_bank, score_bank, probT_bank, o_bank, gate_bank, bias_bank = bank[:7]
        GATE_STRIDE = 16

        def seq(g, c):
            return 4 * g + c

        def tile_no(g, c):
            return 2 * g + c

        def chunk_no(g, c, j=0):
            return 2 * FC * g + FC * c + j

        h1_bank, h3_bank = (bank[0], bank[2]), (bank[1], bank[3])
        y_bank, sa_bank, ba_bank = (bank[4], bank[5]), bank[6], bank[7]

        @block.sync
        def _(sp):
            sp.dma_start(a1_in[:, :], a1.rearrange("e r d -> (e r) d")).then_inc(w_loaded, 16)
            sp.dma_start(a3_in[:, :], a3.rearrange("e r d -> (e r) d")).then_inc(w_loaded, 16)
            sp.dma_start(gate_in[:, :], gate_w).then_inc(w_loaded, 16)
            sp.dma_start(nw[:, :], norm_w.rearrange("(c p) -> p c", p=P),
                         allow_slow_non_contiguous=True).then_inc(w_loaded, 16)
            sp.dma_start(embed_in[:, :], embed).then_inc(w_loaded, 16)
            sp.dma_start(itok_in[:, :], itok.partition_broadcast(STAGES)).then_inc(w_loaded, 16)
            sp.dma_start(w1_in[:, :, :], w1.rearrange("(p j) d -> p j d", j=FC)).then_inc(w_loaded, 16)
            sp.dma_start(w3_in[:, :, :], w3.rearrange("(p j) d -> p j d", j=FC)).then_inc(w_loaded, 16)
            sp.dma_start(b1_in[:, :, :], b1.rearrange("e (p j) r -> p e (j r)", j=FC)).then_inc(w_loaded, 16)
            sp.dma_start(b3_in[:, :, :], b3.rearrange("e (p j) r -> p e (j r)", j=FC)).then_inc(w_loaded, 16)
            sp.dma_start(w2_in[:, :, :], w2.rearrange("(c p) f -> p c f", p=P)).then_inc(w_loaded, 16)
            sp.dma_start(a2_in[:, :], a2.rearrange("e r f -> (e r) f")).then_inc(w_loaded, 16)
            for c in range(DC):
                last = sp.dma_start(b2_in[:, c], b2[:, c * P:(c + 1) * P, :].rearrange("e p r -> p e r"))
                last.then_inc(w_loaded, 16)

            x_rows = x.rearrange("b (h p) d -> (b h) p d", p=P)
            side_rows = side.rearrange("b (h p) d -> (b h) p d", p=P)

            def load(g, c, ring_full=True):
                slot = c % RING
                if ring_full:
                    sp.wait_ge(o_ready, seq(g, c) - RING + 1)
                i = seq(g, c)
                sp.dma_start(x_in[slot][:, :, :], x_rows[bass.ds(SC * i, SC)].rearrange("k p d -> p k d")
                             ).then_inc(seq_loaded[slot], 16)
                sp.dma_start(kv[slot][:, :, :], side_rows[bass.ds(SC * i, SC)].rearrange("k p d -> p k d")
                             ).then_inc(seq_loaded[slot], 16)

            def store(g, c):
                sp.wait_ge(oT_copied, seq(g, c) + 1)
                sp.dma_start(t_scratch[bass.ds(P * seq(g, c), P), :], oT[c % 2][:, :]
                             ).then_inc(t_stored[c % 2], 16)

            for c in range(RING):
                load(0, c, ring_full=False)
            store(0, 0)
            with sp.Fori(0, 7) as g:
                for c in range(2, 6):
                    load(g, c + 2)
                    store(g, c - 1)
            store(0, 29)
            store(0, 30)
            store(0, 31)

            for k in range(2):
                sp.wait_ge(t_stored[k], 16 * BATCH // 2)
            sp.wait_ge(route_done, 1)

            def load_t(g, c, buffer_used=True):
                if buffer_used:
                    sp.wait_ge(t_scaled_ready, tile_no(g, c) - 1)
                sp.dma_start(t_in[c % 2][:, :, :, :].rearrange("p b c s -> p b (c s)"),
                             t_seqs[bass.ds(2 * tile_no(g, c), 2)].rearrange("b p n -> p b n")
                             ).then_inc(t_loaded[c % 2], 16)

            t_seqs = t_scratch.rearrange("(b p) n -> b p n", p=P)
            out_rows = out.rearrange("b (h p) d -> (b h) p d", p=P)

            def load_x(g, c):
                sp.dma_start(x_out[c % 2][:, :, :],
                             x_rows[bass.ds(KT * tile_no(g, c), KT)].rearrange("k p d -> p k d")
                             ).then_inc(x_loaded[c % 2], 16)

            def store_out(g, c):
                sp.wait_ge(out_ready, tile_no(g, c) + 1)
                sp.dma_start(out_rows[bass.ds(KT * tile_no(g, c), KT)].rearrange("k p d -> p k d"),
                             x_out[c % 2][:, :, :]).then_inc(out_stored[c % 2], 16)

            def stored(g, c):
                sp.wait_ge(out_stored[c % 2], 16 * (g + c // 2 + 1))

            load_t(0, 0, buffer_used=False)
            load_x(0, 0)
            load_t(0, 1, buffer_used=False)
            load_x(0, 1)
            with sp.Fori(0, 7) as g:
                for c in (1, 2):
                    load_t(g, c + 1)
                    store_out(g, c - 1)
                    stored(g, c - 1)
                    load_x(g, c + 1)
            store_out(0, TILES - 2)
            store_out(0, TILES - 1)
            stored(0, TILES - 2)
            stored(0, TILES - 1)

        @block.gpsimd
        def _(pool):
            nc.gpsimd.memset(ident[:, :], 0.0).then_inc(const_ready, 1)
            pool.wait_ge(const_ready, 1)
            nc.gpsimd.affine_select(out=ident[:, :], in_=ident[:, :], compare_op=ALU.not_equal, fill=1.0,
                                    base=0, pattern=[[-1, P]], channel_multiplier=1).then_inc(const_ready, 1)
            nc.gpsimd.memset(ones[:, :], 1.0).then_inc(const_ready, 1)
            nc.gpsimd.iota(rank_key[:, :], pattern=[[-1, E]], base=E, channel_multiplier=0,
                           allow_small_or_imprecise_dtypes=True).then_inc(const_ready, 1)
            nc.gpsimd.iota(stage_id[:, :], pattern=[[0, 1]], base=0, channel_multiplier=1,
                           allow_small_or_imprecise_dtypes=True).then_inc(const_ready, 1)

            def t_low(g, c):
                pool.wait_ge(t_hi_ready, tile_no(g, c) + 1)
                nc.gpsimd.tensor_tensor(t_lo[c % 2][:, :, :], t_scaled[:, :, :], f32(t_hi[c % 2][:, :, :]),
                                        ALU.subtract).then_inc(t_lo_ready, 1)

            def v_low(g, c):
                for k in range(4):
                    pool.wait_ge(v_hi_ready, 4 * tile_no(g, c) + k + 1)
                    nc.gpsimd.tensor_tensor(v_lo[k][:, :], v_full[k % 2][:, :], f32(v_hi[k][:, :]),
                                            ALU.subtract).then_inc(v_lo_ready, 1)

            t_low(0, 0)
            v_low(0, 0)
            t_low(0, 1)
            with pool.Fori(0, 7) as g:
                for c in (1, 2):
                    v_low(g, c)
                    t_low(g, c + 1)
            v_low(0, TILES - 1)

        @block.scalar
        def _(act):
            for n, (_, parts) in enumerate(jobs):
                act.wait_ge(wT_ready, n + 1)
                for col, cols, hi, lo, scale in parts:
                    last = nc.scalar.activation(hi, bank[n % 8][:, col:col + cols], ACT.Copy, scale=scale)
                last.then_inc(w_hi_ready, 1)

            def copy_qT(g, c):
                act.wait_ge(qkT_ready, seq(g, c) + 1)
                nc.scalar.activation(qT[c % 2][:, :], qT_bank[:, :], ACT.Copy).then_inc(qT_copied, 1)

            def exp(g, c):
                act.wait_ge(max_ready, seq(g, c) + 1)
                for h in range(SC):
                    last = nc.scalar.activation(prob[c % 2][:, h, :], score_bank[:, h * S:(h + 1) * S], ACT.Exp,
                                                bias=neg_max[c % 2][:, h:h + 1],
                                                accum_out=row_sum[c % RING][:, h:h + 1])
                last.then_inc(prob_ready, 1)

            def copy_oT(g, c, buffer_used=True):
                act.wait_ge(o_ready, seq(g, c) + 1)
                if buffer_used:
                    act.wait_ge(t_stored[c % 2], 16 * (2 * g + c // 2))
                nc.scalar.activation(oT[c % 2][:, :], o_bank[:, :], ACT.Copy).then_inc(oT_copied, 1)
                nc.scalar.activation(oT_sq[c % 2][:, :], o_bank[:, :], ACT.Square).then_inc(oT_squared, 1)

            copy_qT(0, 0)
            exp(0, 0)
            copy_qT(0, 1)
            exp(0, 1)
            copy_qT(0, 2)
            copy_oT(0, 0, buffer_used=False)
            exp(0, 2)
            copy_qT(0, 3)
            copy_oT(0, 1, buffer_used=False)
            exp(0, 3)
            copy_qT(0, 4)
            copy_oT(0, 2)
            with act.Fori(0, 6) as g:
                for c in range(4, 8):
                    exp(g, c)
                    copy_qT(g, c + 1)
                    copy_oT(g, c - 1)
            for c in range(28, 34):
                if c < BATCH:
                    exp(0, c)
                if c + 1 < BATCH:
                    copy_qT(0, c + 1)
                if c - 1 < BATCH:
                    copy_oT(0, c - 1)

            act.wait_ge(gate_read, BATCH)
            nc.scalar.activation(r_y[:, :], mean_sq[:, :], ACT.Sqrt).then_inc(route_act, 1)
            act.wait_ge(route_step, 1)
            nc.scalar.activation(route[:, :, RHO], r_z[:, :], ACT.Exp).then_inc(route_act, 1)

            act.wait_ge(route_done, 1)

            def copy_mask1(g, c):
                act.wait_ge(masks_ready, tile_no(g, c) + 1)
                nc.scalar.activation(mask1[c % 2][:, :], h1_bank[1][:, :], ACT.Copy).then_inc(mask1_copied, 1)

            def copy_rho(g, c):
                act.wait_ge(scales_ready, tile_no(g, c) + 1)
                nc.scalar.activation(rho[c % 2][:, :], h1_bank[0][:, :], ACT.Copy).then_inc(rho_copied, 1)

            def t_high(g, c):
                act.wait_ge(t_scaled_ready, tile_no(g, c) + 1)
                nc.scalar.activation(t_hi[c % 2][:, :, :], t_scaled[:, :, :], ACT.Copy).then_inc(t_hi_ready, 1)

            def v_high(g, c, k):
                act.wait_ge(v_ready, 4 * tile_no(g, c) + k + 1)
                nc.scalar.activation(v_hi[k][:, :], v_full[k % 2][:, :], ACT.Copy).then_inc(v_hi_ready, 1)

            def first_silu(g, c, j):
                act.wait_ge(h1_first, chunk_no(g, c, j) + 1)
                nc.scalar.activation(silu_a[j % 2][:, :], h1_bank[j % 2][:, :], ACT.Silu).then_inc(silu_a_ready, 1)

            def second_silu(g, c, j):
                act.wait_ge(h1_second, chunk_no(g, c, j) + 1)
                nc.scalar.activation(silu_b[j % 2][:, :], h1_bank[j % 2][:, :], ACT.Silu).then_inc(silu_b_ready, 1)

            def down_high(g, c, j, buffer_used=True):
                n = chunk_no(g, c, j)
                if buffer_used:
                    act.wait_ge(down_done, n - 1)
                act.wait_ge(act_s_ready, n + 1)
                nc.scalar.activation(s_hi[j % 2][:, :], act_s[j % 2][:, :], ACT.Copy).then_inc(s_hi_ready, 1)
                act.wait_ge(act_br_ready, n + 1)
                nc.scalar.activation(br_hi[j % 2][:, :], act_br[j % 2][:, :], ACT.Copy).then_inc(br_hi_ready, 1)

            def z_high(g, c):
                act.wait_ge(z_ready, tile_no(g, c) + 1)
                nc.scalar.activation(z_hi[:, :], z_a[:, :], ACT.Copy).then_inc(z_hi_ready, 1)

            def copy_y0(g, c):
                act.wait_ge(y_ready, tile_no(g, c) + 1)
                nc.scalar.activation(yT[:, 0, :], y_bank[0][:, :], ACT.Copy).then_inc(y0_copied, 1)

            def act_tile(g, c, first=False, last=False):
                v_high(g, c, 0)
                v_high(g, c, 1)
                if not first:
                    second_silu(g, c - 1, FC - 1)
                    act.wait_ge(h3_second, chunk_no(g, c))
                v_high(g, c, 2)
                v_high(g, c, 3)
                if not first:
                    down_high(g, c - 1, FC - 1)
                first_silu(g, c, 0)
                if not first:
                    z_high(g, c - 1)
                for j in range(1, FC):
                    first_silu(g, c, j)
                    second_silu(g, c, j - 1)
                    down_high(g, c, j - 1, buffer_used=not (first and j < 3))
                    if j == 1 and not first:
                        copy_y0(g, c - 1)
                    if j == 4 and not last:
                        copy_mask1(g, c + 1)
                    if j == 5 and not last:
                        copy_rho(g, c + 1)
                    if j == 6 and not last:
                        t_high(g, c + 1)

            copy_mask1(0, 0)
            copy_rho(0, 0)
            t_high(0, 0)
            act_tile(0, 0, first=True)
            with act.Fori(0, 7) as g:
                for c in (1, 2):
                    act_tile(g, c)
            act_tile(0, TILES - 1, last=True)
            second_silu(0, TILES - 1, FC - 1)
            down_high(0, TILES - 1, FC - 1)
            z_high(0, TILES - 1)
            copy_y0(0, TILES - 1)

        @block.vector
        def _(dve):
            dve.wait_ge(w_loaded, 16 * W_LOADS)
            dve.wait_ge(const_ready, 5)
            nc.vector.tensor_copy(itok_f[:, :], itok_in[:, :]).then_inc(stage_ready, 1)
            dve.wait_ge(stage_ready, 1)
            nc.vector.tensor_scalar(stage_hot[:, :], itok_f[:, :], stage_id[:, 0:1], None, ALU.is_equal
                                    ).then_inc(stage_ready, 1)
            for src, dst in ((b1_in, b1_by_j), (b3_in, b3_by_j)):
                last = nc.vector.tensor_copy(dst[:, :, :, :].rearrange("p j e r -> p e j r"),
                                             src[:, :, :].rearrange("p e (j r) -> p e j r", j=FC))
            last.then_inc(b_ordered, 1)
            for n, (_, parts) in enumerate(jobs):
                dve.wait_ge(w_hi_ready, n + 1)
                for col, cols, hi, lo, scale in parts:
                    if lo is not None:
                        last = nc.vector.scalar_tensor_tensor(lo, bank[n % 8][:, col:col + cols], scale, f32(hi),
                                                              ALU.mult, ALU.subtract)
                last.then_inc(w_lo_ready, 1)
            dve.wait_ge(bias_ready, 1)
            nc.vector.tensor_copy(bias[:, :, :].rearrange("p h b -> p (h b)"), bias_bank[:, 0:SC * BATCH]
                                  ).then_inc(bias_ready, 1)
            dve.wait_ge(bias_ready, 2)

            def add_bias(g, c, buffer_used=True):
                if buffer_used:
                    dve.wait_ge(qkT_ready, seq(g, c) - 1)
                dve.wait_ge(seq_loaded[c % RING], 32 * (g + c // RING + 1))
                for h in range(SC):
                    last = nc.vector.tensor_scalar(q[c % 2][:, h, :], x_in[c % RING][:, h, :],
                                                   bias[:, h, bass.ds(seq(g, c), 1)], None, ALU.add)
                last.then_inc(q_ready, 1)

            def copy_kT(g, c):
                dve.wait_ge(qkT_ready, seq(g, c) + 1)
                nc.vector.tensor_copy(kT[c % 2][:, :], kT_bank[:, :]).then_inc(kT_copied, 1)

            def row_max(g, c):
                dve.wait_ge(scores_ready, seq(g, c) + 1)
                nc.vector.tensor_reduce(neg_max[c % 2][:, :], score_bank[:, :].rearrange("p (h t) -> p h t", h=SC),
                                        AXIS.X, ALU.max, negate=True).then_inc(max_ready, 1)

            def copy_probT(g, c):
                dve.wait_ge(probT_ready, seq(g, c) + 1)
                nc.vector.tensor_copy(probT[c % 2][:, :], probT_bank[:, :]).then_inc(probT_copied, 1)

            def keep_gate(g, c):
                dve.wait_ge(gate_ready, seq(g, c) + 1)
                r = row_sum[c % RING]
                nc.vector.scalar_tensor_tensor(eps_r2[:, :], r[:, :], EPS, r[:, :], ALU.mult, ALU.mult
                                               ).then_inc(eps_ready, 1)
                dve.wait_ge(eps_ready, seq(g, c) + 1)
                halves = gate_bank[:, 0:SC * GATE_STRIDE].rearrange("p (h n) -> p h n", h=SC)
                nc.vector.scalar_tensor_tensor(mean_sq[:, bass.ds(SC * seq(g, c), SC)], halves[:, :, E], 1.0 / D,
                                               eps_r2[:, :], ALU.mult, ALU.add)
                nc.vector.tensor_scalar(logits[:, bass.ds(SC * seq(g, c), SC), :], halves[:, :, 0:E], 1.0, None,
                                        ALU.mult).then_inc(gate_read, 1)

            add_bias(0, 0, buffer_used=False)
            copy_kT(0, 0)
            add_bias(0, 1, buffer_used=False)

            def dve_step(g, c):
                row_max(g, c)
                copy_kT(g, c + 1)
                add_bias(g, c + 2)
                if not isinstance(g, int) or c >= 2:
                    keep_gate(g, c - 2)
                copy_probT(g, c)

            dve_step(0, 0)
            dve_step(0, 1)
            with dve.Fori(0, 7) as g:
                for c in range(2, 6):
                    dve_step(g, c)
            for c in range(30, 34):
                if c < BATCH:
                    row_max(0, c)
                if c + 1 < BATCH:
                    copy_kT(0, c + 1)
                keep_gate(0, c - 2)
                if c < BATCH:
                    copy_probT(0, c)

            steps = [0]

            def chain(ins):
                steps[0] += 1
                ins.then_inc(route_chain, 1)
                dve.wait_ge(route_chain, steps[0])

            dve.wait_ge(gate_read, BATCH)

            def bcast(ap):
                return ap.unsqueeze(2).to_broadcast([P, COLS, E])

            key = rank_key[:, :].unsqueeze(1).to_broadcast([P, COLS, E])

            def pick(values, best, hot):
                chain(nc.vector.tensor_reduce(best[:, :], values[:, :, :], AXIS.X, ALU.max))
                chain(nc.vector.tensor_tensor(r_eq[:, :, :], values[:, :, :], bcast(best[:, :]), ALU.is_equal))
                chain(nc.vector.tensor_tensor(r_eq[:, :, :], r_eq[:, :, :], key, ALU.mult))
                chain(nc.vector.tensor_reduce(r_key[:, :], r_eq[:, :, :], AXIS.X, ALU.max))
                chain(nc.vector.tensor_tensor(hot, r_eq[:, :, :], bcast(r_key[:, :]), ALU.is_equal))

            hot1 = route[:, :, 0:E]
            pick(logits, top1, hot1)
            chain(nc.vector.scalar_tensor_tensor(r_rest[:, :, :], hot1, -3.0e38, logits[:, :, :],
                                                 ALU.mult, ALU.add))
            pick(r_rest, top2, r_hot2[:, :, :])
            chain(nc.vector.tensor_tensor(route[:, :, DM0:DM0 + E], r_hot2[:, :, :], hot1, ALU.subtract))
            dve.wait_ge(route_act, 1)
            chain(nc.vector.reciprocal(r_t[:, :], r_y[:, :]))
            chain(nc.vector.tensor_tensor(r_z[:, :], r_t[:, :], r_t[:, :], ALU.mult))
            chain(nc.vector.scalar_tensor_tensor(r_z[:, :], r_z[:, :], -0.5, mean_sq[:, :], ALU.mult, ALU.mult))
            chain(nc.vector.scalar_tensor_tensor(route[:, :, RSTD], r_z[:, :], 1.5, r_t[:, :], ALU.add, ALU.mult))
            chain(nc.vector.tensor_tensor(r_z[:, :], top2[:, :], top1[:, :], ALU.subtract))
            nc.vector.tensor_tensor(r_z[:, :], r_z[:, :], route[:, :, RSTD], ALU.mult).then_inc(route_step, 1)
            dve.wait_ge(route_act, 2)
            chain(nc.vector.tensor_scalar(r_t[:, :], route[:, :, RHO], 1.0, None, ALU.add))
            nc.vector.reciprocal(route[:, :, W1ST], r_t[:, :]).then_inc(route_done, 1)
            dve.wait_ge(route_done, 1)

            def load_route(g, c, buffer_used=True):
                if buffer_used:
                    dve.wait_ge(out_ready, tile_no(g, c) - 1)
                cols = bass.ds(KT * tile_no(g, c), KT)
                nc.vector.tensor_scalar(rt[c % 2][:, :, :], route[:, cols, RHO:RHO + 3], 1.0, None, ALU.mult)
                for first, dst in ((0, hot_x), (DM0, hot_dx)):
                    hot = route[:, cols, first:first + E].unsqueeze(3).to_broadcast([P, KT, E, R])
                    last = nc.vector.tensor_scalar(dst[:, :, :, :], hot, 1.0, None, ALU.mult)
                last.then_inc(rt_ready, 1)

            def copy_mask_d(g, c):
                dve.wait_ge(masks_ready, tile_no(g, c) + 1)
                nc.vector.tensor_copy(mask_d[c % 2][:, :], h3_bank[1][:, :]).then_inc(mask_d_copied, 1)

            def scale_t(g, c, buffer_used=True):
                dve.wait_ge(scales_ready, tile_no(g, c) + 1)
                dve.wait_ge(t_loaded[c % 2], 16 * (g + c // 2 + 1))
                if buffer_used:
                    dve.wait_ge(t_lo_ready, tile_no(g, c))
                for dc in range(DC):
                    last = nc.vector.tensor_tensor(t_scaled[:, dc, :].rearrange("p (b s) -> p b s", b=2),
                                                   t_in[c % 2][:, :, dc, :],
                                                   h3_bank[0][:, :].rearrange("p (b s) -> p b s", b=2), ALU.mult)
                last.then_inc(t_scaled_ready, 1)

            def mask_u(g, c, first=False):
                dve.wait_ge(u_ready, tile_no(g, c) + 1)
                dve.wait_ge(mask1_copied, tile_no(g, c) + 1)
                dve.wait_ge(mask_d_copied, tile_no(g, c) + 1)
                for k in range(4):
                    if not (first and k < 2):
                        dve.wait_ge(v_lo_ready, 4 * tile_no(g, c) + k - 1)
                    u = (h1_bank[0], h3_bank[0])[k % 2]
                    m = (mask1, mask_d)[k // 2][c % 2]
                    nc.vector.tensor_tensor(v_full[k % 2][:, :], u[:, :], m[:, :], ALU.mult).then_inc(v_ready, 1)

            def first_act(g, c, j):
                dve.wait_ge(h3_first, chunk_no(g, c, j) + 1)
                dve.wait_ge(silu_a_ready, chunk_no(g, c, j) + 1)
                nc.vector.tensor_tensor(act_a[j % 2][:, :], silu_a[j % 2][:, :], h3_bank[j % 2][:, :], ALU.mult
                                        ).then_inc(act_a_ready, 1)

            def second_act(g, c, j):
                n = chunk_no(g, c, j)
                dve.wait_ge(h3_second, n + 1)
                dve.wait_ge(silu_b_ready, n + 1)
                nc.vector.tensor_tensor(act_b[:, :], silu_b[j % 2][:, :], h3_bank[j % 2][:, :], ALU.mult
                                        ).then_inc(act_b_ready, 1)
                if j == 0:
                    dve.wait_ge(rho_copied, tile_no(g, c) + 1)
                dve.wait_ge(act_b_ready, n + 1)
                nc.vector.tensor_tensor(act_br[j % 2][:, :], act_b[:, :], rho[c % 2][:, :], ALU.mult
                                        ).then_inc(act_br_ready, 1)
                dve.wait_ge(act_br_ready, n + 1)
                dve.wait_ge(act_a_ready, n + 1)
                nc.vector.tensor_tensor(act_s[j % 2][:, :], act_a[j % 2][:, :], act_br[j % 2][:, :], ALU.add
                                        ).then_inc(act_s_ready, 1)

            def down_low(g, c, j):
                n = chunk_no(g, c, j)
                dve.wait_ge(s_hi_ready, n + 1)
                nc.vector.tensor_tensor(s_lo[j % 2][:, :], act_s[j % 2][:, :], f32(s_hi[j % 2][:, :]), ALU.subtract)
                dve.wait_ge(br_hi_ready, n + 1)
                nc.vector.tensor_tensor(br_lo[j % 2][:, :], act_br[j % 2][:, :], f32(br_hi[j % 2][:, :]), ALU.subtract
                                        ).then_inc(down_in_ready, 1)

            def mask_z(g, c):
                n = tile_no(g, c) + 1
                dve.wait_ge(down_done, chunk_no(g, c, FC))
                nc.vector.tensor_tensor(z_b[:, :], ba_bank[:, :], mask_d[c % 2][:, :], ALU.mult).then_inc(z_b_ready, 1)
                nc.vector.tensor_tensor(z_a[:, :], sa_bank[:, :], mask1[c % 2][:, :], ALU.mult).then_inc(z_a_ready, 1)
                dve.wait_ge(z_b_ready, n)
                dve.wait_ge(z_a_ready, n)
                nc.vector.tensor_tensor(z_a[:, :], z_a[:, :], z_b[:, :], ALU.add).then_inc(z_ready, 1)
                dve.wait_ge(z_hi_ready, n)
                nc.vector.tensor_tensor(z_lo[:, :], z_a[:, :], f32(z_hi[:, :]), ALU.subtract).then_inc(z_lo_ready, 1)

            def copy_y1(g, c):
                dve.wait_ge(y_ready, tile_no(g, c) + 1)
                nc.vector.tensor_copy(yT[:, 1, :], y_bank[1][:, :]).then_inc(y1_copied, 1)

            def add_residual(g, c):
                dve.wait_ge(yT_ready, tile_no(g, c) + 1)
                dve.wait_ge(x_loaded[c % 2], 16 * (g + c // 2 + 1))
                for k in range(KT):
                    y = (h1_bank[0], h3_bank[0])[k // 2][:, (k % 2) * D:(k % 2 + 1) * D]
                    last = nc.vector.scalar_tensor_tensor(x_out[c % 2][:, k, :], y, rt[c % 2][:, k, W1ST - RHO:W1ST - RHO + 1],
                                                          x_out[c % 2][:, k, :], ALU.mult, ALU.add)
                last.then_inc(out_ready, 1)

            def dve_tile(g, c, first=False, last=False):
                mask_u(g, c, first)
                if not first:
                    second_act(g, c - 1, FC - 1)
                    down_low(g, c - 1, FC - 1)
                first_act(g, c, 0)
                if not first:
                    mask_z(g, c - 1)
                for j in range(1, FC):
                    first_act(g, c, j)
                    second_act(g, c, j - 1)
                    if j == 3 and not first:
                        add_residual(g, c - 1)
                    if j == 4 and not last:
                        copy_mask_d(g, c + 1)
                    if j == 5 and not last:
                        scale_t(g, c + 1)
                    down_low(g, c, j - 1)
                    if j == 1 and not first:
                        copy_y1(g, c - 1)
                    if j == 3 and not last:
                        load_route(g, c + 1, buffer_used=not first)

            load_route(0, 0, buffer_used=False)
            copy_mask_d(0, 0)
            scale_t(0, 0, buffer_used=False)
            dve_tile(0, 0, first=True)
            with dve.Fori(0, 7) as g:
                for c in (1, 2):
                    dve_tile(g, c)
            dve_tile(0, TILES - 1, last=True)
            second_act(0, TILES - 1, FC - 1)
            down_low(0, TILES - 1, FC - 1)
            mask_z(0, TILES - 1)
            copy_y1(0, TILES - 1)
            add_residual(0, TILES - 1)

        @block.tensor
        def _(pe):
            pe.wait_ge(const_ready, 5)
            pe.wait_ge(w_loaded, 16 * W_LOADS)
            pe.wait_ge(b_ordered, 1)
            for n, (pieces, _) in enumerate(jobs):
                if n >= 8:
                    pe.wait_ge(w_lo_ready, n - 7)
                for col, cols, src, rows in pieces:
                    last = nc.tensor.transpose(bank[n % 8][0:P, col:col + cols], src, ident[0:rows, 0:rows])
                last.then_inc(wT_ready, 1)
            pe.wait_ge(stage_ready, 2)
            pe.wait_ge(w_lo_ready, JOBS)
            for h in range(SC):
                last = nc.tensor.matmul(bias_bank[:, h * BATCH:(h + 1) * BATCH], embed_in[:, h * P:(h + 1) * P],
                                        stage_hot[:, :], start=True, stop=True)
            last.then_inc(bias_ready, 1)

            def transpose_qk(g, c):
                pe.wait_ge(q_ready, seq(g, c) + 1)
                for src, dst in ((q[c % 2], qT_bank), (kv[c % RING], kT_bank)):
                    for dc in range(DC):
                        for h in range(SC):
                            last = nc.tensor.transpose(dst[:, dc * S + h * P:dc * S + (h + 1) * P],
                                                       src[:, h, dc * P:(dc + 1) * P], ident[:, :])
                last.then_inc(qkT_ready, 1)

            def scores(g, c):
                pe.wait_ge(qT_copied, seq(g, c) + 1)
                pe.wait_ge(kT_copied, seq(g, c) + 1)
                for h in range(SC):
                    for dc in range(DC):
                        last = nc.tensor.matmul(score_bank[:, h * S:(h + 1) * S],
                                                qT[c % 2][:, dc * S + h * P:dc * S + (h + 1) * P],
                                                kT[c % 2][:, dc * S:(dc + 1) * S],
                                                start=(dc == 0), stop=(dc == DC - 1))
                last.then_inc(scores_ready, 1)

            def transpose_prob(g, c):
                pe.wait_ge(prob_ready, seq(g, c) + 1)
                for tc in range(SC):
                    for h in range(SC):
                        last = nc.tensor.transpose(probT_bank[:, tc * S + h * P:tc * S + (h + 1) * P],
                                                   prob[c % 2][:, h, tc * P:(tc + 1) * P], ident[:, :])
                last.then_inc(probT_ready, 1)

            def attend(g, c):
                pe.wait_ge(probT_copied, seq(g, c) + 1)
                for dc in range(DC):
                    for tc in range(SC):
                        last = nc.tensor.matmul(o_bank[:, dc * S:(dc + 1) * S],
                                                kv[c % RING][:, tc, dc * P:(dc + 1) * P],
                                                probT[c % 2][:, tc * S:(tc + 1) * S],
                                                start=(tc == 0), stop=(tc == SC - 1))
                last.then_inc(o_ready, 1)

            def gate(g, c, bank_used=True):
                pe.wait_ge(oT_copied, seq(g, c) + 1)
                pe.wait_ge(oT_squared, seq(g, c) + 1)
                if bank_used:
                    pe.wait_ge(gate_read, seq(g, c))
                for h in range(SC):
                    col = h * GATE_STRIDE
                    for dc in range(DC):
                        nc.tensor.matmul(gate_bank[:, col:col + E], oT[c % 2][:, dc * S + h * P:dc * S + (h + 1) * P],
                                         gateT[:, dc, :], start=(dc == 0), stop=(dc == DC - 1))
                    for dc in range(DC):
                        last = nc.tensor.matmul(gate_bank[:, col + E:col + E + 1],
                                                oT_sq[c % 2][:, dc * S + h * P:dc * S + (h + 1) * P],
                                                ones[:, :], start=(dc == 0), stop=(dc == DC - 1))
                last.then_inc(gate_ready, 1)

            transpose_qk(0, 0)
            scores(0, 0)
            transpose_qk(0, 1)
            transpose_prob(0, 0)
            scores(0, 1)
            transpose_qk(0, 2)
            attend(0, 0)
            transpose_prob(0, 1)
            scores(0, 2)
            transpose_qk(0, 3)
            gate(0, 0, bank_used=False)
            attend(0, 1)
            transpose_prob(0, 2)

            def pe_step(g, c):
                scores(g, c)
                transpose_qk(g, c + 1)
                gate(g, c - 2)
                attend(g, c - 1)
                transpose_prob(g, c)

            pe_step(0, 3)
            with pe.Fori(0, 6) as g:
                for c in range(4, 8):
                    pe_step(g, c)
            pe_step(0, 28)
            pe_step(0, 29)
            pe_step(0, 30)
            scores(0, 31)
            gate(0, 29)
            attend(0, 30)
            transpose_prob(0, 31)
            gate(0, 30)
            attend(0, 31)
            gate(0, 31)

            def product(dst, w, x_parts, start, stop, grouped=True):
                (w_hi, w_lo), (x_hi, x_lo) = w, x_parts
                nc.tensor.matmul(dst, w_hi, x_hi, start=start, stop=False, skip_group_check=not grouped)
                nc.tensor.matmul(dst, w_hi, x_lo, start=False, stop=False, skip_group_check=not grouped)
                return nc.tensor.matmul(dst, w_lo, x_hi, start=False, stop=stop, skip_group_check=not grouped)

            def at(parts, *index):
                return parts[0][index], parts[1][index]

            ALL = slice(None)

            def prep_masks(g, c):
                pe.wait_ge(rt_ready, tile_no(g, c) + 1)
                for dst, hot in ((h1_bank[1], hot_x), (h3_bank[1], hot_dx)):
                    for k in range(KT):
                        last = nc.tensor.transpose(dst[:, k * P:(k + 1) * P],
                                                   hot[:, k].rearrange("p e r -> p (e r)"), ident[:, :])
                last.then_inc(masks_ready, 1)

            def prep_scales(g, c):
                pe.wait_ge(rt_ready, tile_no(g, c) + 1)
                for dst, col in ((h1_bank[0], 0), (h3_bank[0], RSTD - RHO)):
                    for k in range(KT):
                        last = nc.tensor.transpose(dst[:, k * P:(k + 1) * P],
                                                   rt[c % 2][:, k, col:col + 1].to_broadcast([P, P]), ident[:, :])
                last.then_inc(scales_ready, 1)

            def low_rank(g, c):
                pe.wait_ge(t_lo_ready, tile_no(g, c) + 1)
                for w, dst in ((0, h1_bank[0]), (1, h3_bank[0])):
                    for dc in range(DC):
                        last = product(dst[:, :], at(a13T, ALL, dc, w), (t_hi[c % 2][:, dc], t_lo[c % 2][:, dc]),
                                       dc == 0, dc == DC - 1)
                last.then_inc(u_ready, 1)

            def first_expert(g, c, j):
                f = slice(j * P, (j + 1) * P)
                for wT, bT, dst, k, done in ((w1T, b1T, h1_bank[j % 2], 0, h1_first),
                                             (w3T, b3T, h3_bank[j % 2], 1, h3_first)):
                    for dc in range(DC):
                        product(dst[:, :], at(wT, ALL, dc, f), (t_hi[c % 2][:, dc], t_lo[c % 2][:, dc]), dc == 0, False)
                    if j == 0:
                        pe.wait_ge(v_lo_ready, 4 * tile_no(g, c) + k + 1)
                    product(dst[:, :], at(bT, ALL, f), (v_hi[k][:, :], v_lo[k][:, :]), False, True).then_inc(done, 1)

            def second_expert(g, c, j):
                if j == 0:
                    pe.wait_ge(v_lo_ready, 4 * tile_no(g, c) + 4)
                pe.wait_ge(act_a_ready, chunk_no(g, c, j) + 1)
                f = slice(j * P, (j + 1) * P)
                for bT, dst, k, done in ((b1T, h1_bank[j % 2], 2, h1_second), (b3T, h3_bank[j % 2], 3, h3_second)):
                    product(dst[:, :], at(bT, ALL, f), (v_hi[k][:, :], v_lo[k][:, :]), False, True, grouped=False
                            ).then_inc(done, 1)

            def down_s(g, c, j):
                pe.wait_ge(down_in_ready, chunk_no(g, c, j) + 1)
                s = (s_hi[j % 2][:, :], s_lo[j % 2][:, :])
                for half in range(DC):
                    product(y_bank[half][:, :], at(w2T, ALL, j, slice(half * P, (half + 1) * P)), s, j == 0, False)
                product(sa_bank[:, :], at(a2T, ALL, j), s, j == 0, j == FC - 1)

            def down_b(g, c, j):
                product(ba_bank[:, :], at(a2T, ALL, j), (br_hi[j % 2][:, :], br_lo[j % 2][:, :]), j == 0, j == FC - 1
                        ).then_inc(down_done, 1)

            def finish_y(g, c):
                pe.wait_ge(z_lo_ready, tile_no(g, c) + 1)
                for half in range(DC):
                    last = product(y_bank[half][:, :], at(b2T, ALL, slice(half * P, (half + 1) * P)),
                                   (z_hi[:, :], z_lo[:, :]), False, True)
                last.then_inc(y_ready, 1)

            def transpose_y(g, c):
                pe.wait_ge(y0_copied, tile_no(g, c) + 1)
                pe.wait_ge(y1_copied, tile_no(g, c) + 1)
                for k in range(KT):
                    dst = (h1_bank[0], h3_bank[0])[k // 2]
                    for half in range(DC):
                        col = (k % 2) * D + half * P
                        last = nc.tensor.transpose(dst[:, col:col + P], yT[:, half, k * P:(k + 1) * P], ident[:, :])
                last.then_inc(yT_ready, 1)

            def pe_tile(g, c, first=False, last=False):
                n = chunk_no(g, c)
                if not first:
                    pe.wait_ge(act_b_ready, n - 1)
                low_rank(g, c)
                if not first:
                    second_expert(g, c - 1, FC - 1)
                    down_s(g, c - 1, FC - 2)
                    down_b(g, c - 1, FC - 2)
                pe.wait_ge(v_ready, 4 * tile_no(g, c) + 4)
                first_expert(g, c, 0)
                if not first:
                    down_s(g, c - 1, FC - 1)
                    down_b(g, c - 1, FC - 1)
                for j in range(1, FC):
                    if j == 4 and not first:
                        pe.wait_ge(out_ready, tile_no(g, c))
                    elif j == 5 and not last:
                        pe.wait_ge(mask1_copied, tile_no(g, c) + 2)
                        pe.wait_ge(mask_d_copied, tile_no(g, c) + 2)
                    elif j == 6 and not last:
                        pe.wait_ge(rho_copied, tile_no(g, c) + 2)
                        pe.wait_ge(t_scaled_ready, tile_no(g, c) + 2)
                    elif not (first and j == 1):
                        pe.wait_ge(act_b_ready, n + j - 1)
                    first_expert(g, c, j)
                    if j == 2 and not first:
                        finish_y(g, c - 1)
                    second_expert(g, c, j - 1)
                    if j == 2 and not first:
                        pe.wait_ge(y0_copied, tile_no(g, c))
                        pe.wait_ge(y1_copied, tile_no(g, c))
                    if j >= 2:
                        down_s(g, c, j - 2)
                    if j == 3 and not first:
                        pe.wait_ge(act_b_ready, n + 3)
                        transpose_y(g, c - 1)
                    if j == 4 and not last:
                        pe.wait_ge(act_b_ready, n + 4)
                        prep_masks(g, c + 1)
                    if j == 5 and not last:
                        pe.wait_ge(act_b_ready, n + 5)
                        prep_scales(g, c + 1)
                    if j >= 2:
                        down_b(g, c, j - 2)

            pe.wait_ge(route_done, 1)
            prep_masks(0, 0)
            prep_scales(0, 0)
            pe.wait_ge(mask1_copied, 1)
            pe.wait_ge(mask_d_copied, 1)
            pe.wait_ge(rho_copied, 1)
            pe.wait_ge(t_scaled_ready, 1)
            pe_tile(0, 0, first=True)
            with pe.Fori(0, 7) as g:
                for c in (1, 2):
                    pe_tile(g, c)
            end = TILES - 1
            pe_tile(0, end, last=True)
            second_expert(0, end, FC - 1)
            for j in (FC - 2, FC - 1):
                down_s(0, end, j)
                down_b(0, end, j)
            finish_y(0, end)
            pe.wait_ge(act_b_ready, chunk_no(0, end, FC))
            transpose_y(0, end)


_INS = ['x', 'fside_BxSxS_0', 'itok_B_0_5', 'L0_cond_braak_embed', 'L0_ffn_norm_w', 'L0_ffn_w1', 'L0_ffn_w3',
        'L0_ffn_w2', 'L0_ffn_gate_w', 'L0_ffn_a1', 'L0_ffn_b1', 'L0_ffn_a3', 'L0_ffn_b3', 'L0_ffn_a2', 'L0_ffn_b2']


def kernel(**inputs):
    import numpy as np
    import concourse.bacc as bacc
    from concourse.bass_utils import run_bass_kernel_spmd

    nc = bacc.Bacc("TRN2", target_bir_lowering=False, num_devices=1)
    arrays, args = {}, []
    for name in _INS:
        a = np.ascontiguousarray(inputs[name])
        arrays[f"in_{name}"] = a
        args.append(nc.dram_tensor(f"in_{name}", a.shape, mybir.dt.from_np(a.dtype), kind="ExternalInput").ap())
    args.append(nc.dram_tensor("out_0", (BATCH, S, D), F32, kind="ExternalOutput").ap())
    adaln_moe_ffn(nc, *args)
    r = run_bass_kernel_spmd(nc, [arrays], core_ids=[0])
    return r.results[0]["out_0"]
```

```python
from contextlib import ExitStack

import concourse.bass as bass
from concourse import mybir
from concourse.alu_op_type import AluOpType as ALU

F32 = mybir.dt.float32
F32R = mybir.dt.float32r
BF16 = mybir.dt.bfloat16
I32 = mybir.dt.int32
ACT = mybir.ActivationFunctionType
AXIS = mybir.AxisListType

P = 128
BATCH, S, D = 32, 256, 256
F, E, R = 1024, 8, 16
STAGES = 6
ER = E * R
SC = S // P
DC = D // P
FC = F // P
TILE = 512
KT = TILE // P
TILES = BATCH * S // TILE
COLS = BATCH * SC
SCALING = 32.0 / 16.0
EPS = 1e-06
RING = 4
GROUP = 4
GCOLS = GROUP * SC
RSQRT_SEED = float(0x5F3759DF)


def adaln_moe_ffn(nc, x, side, itok, embed, norm_w, w1, w3, w2, gate_w, a1, b1, a3, b3, a2, b2, out):
    ctx = ExitStack()
    with ctx:
        def sem(name):
            return ctx.enter_context(nc.semaphore(name))

        def sems(name, n):
            return [sem(f"{name}{k}") for k in range(n)]

        def sb(stack, name, shape, dt=F32):
            return stack.enter_context(nc.sbuf_tensor(name, shape, dt))

        bank = [ctx.enter_context(nc.psum_tensor(f"bank{k}", [P, 512], F32)) for k in range(8)]
        t_scratch = nc.dram_tensor("t_scratch", [BATCH * P, DC * S], F32, kind="Internal").ap()
        hot_scratch = nc.dram_tensor("hot_scratch", [2, E, COLS, P], BF16, kind="Internal").ap()
        scale_scratch = nc.dram_tensor("scale_scratch", [2, COLS, P], F32, kind="Internal").ap()

        ident = sb(ctx, "ident", [P, P])
        ones = sb(ctx, "ones", [P, 1])
        rank_key = sb(ctx, "rank_key", [P, E])
        stage_id = sb(ctx, "stage_id", [STAGES, 1])

        def split(name, shape, stack=ctx):
            return sb(stack, name + "_hi", shape, F32R), sb(stack, name + "_lo", shape, F32R)

        w1T = split("w1T", [P, DC, F])
        w3T = split("w3T", [P, DC, F])
        w2T = split("w2T", [P, FC, D])
        a2T = split("a2T", [P, FC, ER])
        a13T = split("a13T", [P, DC, 2, ER])
        b1T = split("b1T", [ER, F])
        b3T = split("b3T", [ER, F])
        b2T = split("b2T", [ER, D])
        gateT = sb(ctx, "gateT", [P, DC, E])
        w_first = sb(ctx, "w_first", [P, COLS])
        logits = sb(ctx, "logits", [P, GCOLS, E])
        mean_sq = sb(ctx, "mean_sq", [P, GCOLS])
        row_sum = [sb(ctx, f"row_sum{k}", [P, SC]) for k in range(RING)]
        eps_r2 = sb(ctx, "eps_r2", [P, SC])
        g_logits = sb(ctx, "g_logits", [P, GCOLS, E])
        g_z = sb(ctx, "g_z", [P, GCOLS])
        g_top1 = sb(ctx, "g_top1", [P, GCOLS])
        g_top2 = sb(ctx, "g_top2", [P, GCOLS])
        g_best = sb(ctx, "g_best", [P, GCOLS])
        g_key = sb(ctx, "g_key", [P, GCOLS, E])
        g_hot1 = sb(ctx, "g_hot1", [P, GCOLS, E])
        g_hot2 = sb(ctx, "g_hot2", [P, GCOLS, E])
        g_y = sb(ctx, "g_y", [P, GCOLS])
        g_t = sb(ctx, "g_t", [P, GCOLS])
        hots = sb(ctx, "hots", [P, 2, E, GCOLS])
        scales = sb(ctx, "scales", [P, 2, GCOLS])
        hot_rows = sb(ctx, "hot_rows", [2 * GCOLS * E, P], BF16)
        scale_rows = sb(ctx, "scale_rows", [2 * GCOLS, P])
        gate_in = sb(ctx, "gate_in", [E, D])
        nw = sb(ctx, "nw", [P, DC])
        bias = sb(ctx, "bias", [P, SC, BATCH])
        neg_max = [sb(ctx, f"neg_max{k}", [P, SC]) for k in range(2)]
        embed_in = sb(ctx, "embed_in", [STAGES, S])
        itok_in = sb(ctx, "itok_in", [STAGES, BATCH], I32)
        itok_f = sb(ctx, "itok_f", [STAGES, BATCH])
        stage_hot = sb(ctx, "stage_hot", [STAGES, BATCH])

        early = ExitStack()
        w1_in = sb(early, "w1_in", [P, FC, D])
        w3_in = sb(early, "w3_in", [P, FC, D])
        w2_in = sb(early, "w2_in", [P, DC, F])
        b1_in = sb(early, "b1_in", [P, E, FC * R])
        b3_in = sb(early, "b3_in", [P, E, FC * R])
        b1_by_j = sb(early, "b1_by_j", [P, FC, E, R])
        b3_by_j = sb(early, "b3_by_j", [P, FC, E, R])
        a1_in = sb(early, "a1_in", [ER, D])
        a3_in = sb(early, "a3_in", [ER, D])
        a2_in = sb(early, "a2_in", [ER, F])
        b2_in = sb(early, "b2_in", [P, DC, E, R])
        x_in = [sb(early, f"x_in{k}", [P, SC, D]) for k in range(RING)]
        kv = [sb(early, f"kv{k}", [P, SC, D]) for k in range(RING)]
        q = [sb(early, f"q{k}", [P, SC, D]) for k in range(2)]
        qT = [split(f"qT{k}", [P, DC * S], early) for k in range(2)]
        kT = [split(f"kT{k}", [P, DC * S], early) for k in range(2)]
        prob = [sb(early, f"prob{k}", [P, SC, S]) for k in range(2)]
        value = [split(f"value{k}", [P, SC, D], early) for k in range(2)]
        probT = [split(f"probT{k}", [P, SC * S], early) for k in range(2)]
        oT = [sb(early, f"oT{k}", [P, DC * S]) for k in range(2)]
        oT_sq = [sb(early, f"oT_sq{k}", [P, DC * S]) for k in range(2)]
        sq_sum = [sb(early, f"sq_sum{k}", [P, S]) for k in range(2)]
        early.close()

        late = ctx
        t_in = [sb(late, f"t_in{k}", [P, 2, DC, S]) for k in range(2)]
        t_scaled = sb(late, "t_scaled", [P, DC, TILE])
        t_hi = [sb(late, f"t_hi{k}", [P, DC, TILE], F32R) for k in range(2)]
        t_lo = [sb(late, f"t_lo{k}", [P, DC, TILE], F32R) for k in range(2)]
        mask1 = [sb(late, f"mask1_{k}", [ER, TILE], BF16) for k in range(2)]
        mask_d = [sb(late, f"mask_d{k}", [ER, TILE], BF16) for k in range(2)]
        rho = [sb(late, f"rho{k}", [P, TILE]) for k in range(2)]
        rstd = [sb(late, f"rstd{k}", [P, TILE]) for k in range(2)]
        v_full = [sb(late, f"v_full{k}", [ER, TILE]) for k in range(4)]
        v_hi = [sb(late, f"v_hi{k}", [ER, TILE], F32R) for k in range(4)]
        v_lo = [sb(late, f"v_lo{k}", [ER, TILE], F32R) for k in range(4)]
        silu_a = [sb(late, f"silu_a{k}", [P, TILE]) for k in range(2)]
        silu_b = sb(late, "silu_b", [P, TILE])
        act_a = [sb(late, f"act_a{k}", [P, TILE]) for k in range(2)]
        act_b = sb(late, "act_b", [P, TILE])
        act_br = [sb(late, f"act_br{k}", [P, TILE]) for k in range(2)]
        act_s = [sb(late, f"act_s{k}", [P, TILE]) for k in range(2)]
        s_hi = [sb(late, f"s_hi{k}", [P, TILE], F32R) for k in range(2)]
        s_lo = [sb(late, f"s_lo{k}", [P, TILE], F32R) for k in range(2)]
        br_hi = [sb(late, f"br_hi{k}", [P, TILE], F32R) for k in range(2)]
        br_lo = [sb(late, f"br_lo{k}", [P, TILE], F32R) for k in range(2)]
        z_a = sb(late, "z_a", [ER, TILE])
        z_b = sb(late, "z_b", [ER, TILE])
        z_hi = sb(late, "z_hi", [ER, TILE], F32R)
        z_lo = sb(late, "z_lo", [ER, TILE], F32R)
        yT = sb(late, "yT", [P, DC, TILE])
        y_scaled = sb(late, "y_scaled", [P, KT // 2, D])
        rt = [sb(late, f"rt{k}", [P, KT]) for k in range(2)]
        x_out = [sb(late, f"x_out{k}", [P, KT, D]) for k in range(2)]

        const_ready = sem("const_ready")
        small_loaded = sem("small_loaded")
        w_loaded = sem("w_loaded")
        stage_ready = sem("stage_ready")
        gate_wT_ready = sem("gate_wT_ready")
        gate_w_copied = sem("gate_w_copied")
        b_ordered = sem("b_ordered")
        wT_ready = sem("wT_ready")
        w_hi_ready = sem("w_hi_ready")
        w_lo_ready = sem("w_lo_ready")
        bias_ready = sem("bias_ready")
        bias_copied = sem("bias_copied")
        seq_loaded = sems("seq_loaded", RING)
        q_ready = sem("q_ready")
        qkT_ready = sem("qkT_ready")
        qT_hi_ready = sem("qT_hi_ready")
        kT_hi_ready = sem("kT_hi_ready")
        qkT_lo_ready = sem("qkT_lo_ready")
        scores_ready = sem("scores_ready")
        max_ready = sem("max_ready")
        prob_ready = sem("prob_ready")
        value_hi_ready = sem("value_hi_ready")
        value_lo_ready = sem("value_lo_ready")
        probT_ready = sem("probT_ready")
        probT_hi_ready = sem("probT_hi_ready")
        probT_lo_ready = sem("probT_lo_ready")
        o_ready = sem("o_ready")
        oT_copied = sem("oT_copied")
        oT_squared = sem("oT_squared")
        sq_summed = sem("sq_summed")
        gate_ready = sem("gate_ready")
        eps_ready = sem("eps_ready")
        gate_read = sem("gate_read")
        t_stored = sems("t_stored", 2)
        route_chain = sem("route_chain")
        gap_ready = sem("gap_ready")
        rho_ready = sem("rho_ready")
        scales_ready = sem("scales_ready")
        rows_ready = sem("rows_ready")
        rows_copied = sem("rows_copied")
        rows_stored = sem("rows_stored")

        tile_loaded = sems("tile_loaded", 2)
        x_loaded = sems("x_loaded", 2)
        out_stored = sems("out_stored", 2)
        rt_ready = sem("rt_ready")
        t_scaled_ready = sem("t_scaled_ready")
        t_hi_ready = sem("t_hi_ready")
        t_lo_ready = sem("t_lo_ready")
        u_ready = sem("u_ready")
        v_ready = sem("v_ready")
        v_hi_ready = sem("v_hi_ready")
        v_lo_ready = sem("v_lo_ready")
        h1_first = sem("h1_first")
        h3_first = sem("h3_first")
        h1_second = sem("h1_second")
        h3_second = sem("h3_second")
        silu_a_ready = sem("silu_a_ready")
        silu_b_ready = sem("silu_b_ready")
        act_a_ready = sem("act_a_ready")
        act_b_ready = sem("act_b_ready")
        act_br_ready = sem("act_br_ready")
        act_s_ready = sem("act_s_ready")
        s_hi_ready = sem("s_hi_ready")
        br_hi_ready = sem("br_hi_ready")
        down_in_ready = sem("down_in_ready")
        down_done = sem("down_done")
        z_in_ready = sem("z_in_ready")
        z_a_ready = sem("z_a_ready")
        z_b_ready = sem("z_b_ready")
        z_ready = sem("z_ready")
        z_hi_ready = sem("z_hi_ready")
        z_lo_ready = sem("z_lo_ready")
        y_ready = sem("y_ready")
        y0_copied = sem("y0_copied")
        y1_copied = sem("y1_copied")
        yT_ready = sem("yT_ready")
        y_scaled_ready = sem("y_scaled_ready")
        out_a_ready = sem("out_a_ready")
        out_b_ready = sem("out_b_ready")

        block = ctx.enter_context(nc.Block())

        def f32(ap):
            return ap.bitcast(F32)

        jobs = []

        def nw_at(c):
            return nw[:, c:c + 1]

        a13_in = (a1_in, a3_in)
        jobs.append(([(128 * (2 * c + w), 128, a13_in[w][:, c * P:(c + 1) * P], ER)
                      for c in range(DC) for w in range(2)],
                     [(256 * c, 256, a13T[0][:, c].rearrange("p w e -> p (w e)"),
                       a13T[1][:, c].rearrange("p w e -> p (w e)"), nw_at(c)) for c in range(DC)]))
        for src, dst in ((w1_in, w1T), (w3_in, w3T)):
            for c in range(DC):
                for j0 in range(0, FC, 4):
                    jobs.append(([(128 * k, 128, src[:, j0 + k, c * P:(c + 1) * P], P) for k in range(4)],
                                 [(0, 512, dst[0][:, c, j0 * P:(j0 + 4) * P],
                                   dst[1][:, c, j0 * P:(j0 + 4) * P], nw_at(c))]))
        for src, dst in ((b1_by_j, b1T), (b3_by_j, b3T)):
            for j0 in range(0, FC, 4):
                jobs.append(([(128 * k, 128, src[:, j0 + k].rearrange("p e r -> p (e r)"), P) for k in range(4)],
                             [(0, 512, dst[0][:, j0 * P:(j0 + 4) * P],
                               dst[1][:, j0 * P:(j0 + 4) * P], SCALING)]))
        for j0 in range(0, FC, 2):
            jobs.append(([(128 * (2 * k + c), 128, w2_in[:, c, j0 + k:F:FC], P)
                          for k in range(2) for c in range(DC)],
                         [(0, 512, w2T[0][:, j0:j0 + 2].rearrange("p j d -> p (j d)"),
                           w2T[1][:, j0:j0 + 2].rearrange("p j d -> p (j d)"), 1.0)]))
        for j0 in range(0, FC, 4):
            jobs.append(([(128 * k, 128, a2_in[:, j0 + k:F:FC], ER) for k in range(4)],
                         [(0, 512, a2T[0][:, j0:j0 + 4].rearrange("p j e -> p (j e)"),
                           a2T[1][:, j0:j0 + 4].rearrange("p j e -> p (j e)"), 1.0)]))
        jobs.append(([(128 * c, 128, b2_in[:, c].rearrange("p e r -> p (e r)"), P) for c in range(DC)],
                     [(0, 256, b2T[0][:, :], b2T[1][:, :], SCALING)]))
        JOBS = len(jobs)
        JOB_STEPS = range(4, 8)
        JOBS_PER_STEP = JOBS // len(JOB_STEPS)
        W_LOADS, SMALL_LOADS = 10, 4
        TILE_LOADS = 16 * 5

        def job_no(i, k):
            return (i - JOB_STEPS[0]) * JOBS_PER_STEP + k

        qT_bank, kT_bank, score_bank, probT_bank, o_bank, gate_bank, row_bank, bias_bank = bank
        w_bank = bank[6:8]
        GATE_STRIDE = 16

        def seq(g, c):
            return 4 * g + c

        def group_of(g, c, lag):
            return g + (c - lag) // GROUP

        HEAD, TAIL = range(0, 12), range(28, 32)
        LOOP = range(12, 16)
        LOOPS = (TAIL[0] - LOOP[0]) // 4

        def tile_no(g, c):
            return 2 * g + c

        def chunk_no(g, c, j=0):
            return 2 * FC * g + FC * c + j

        h1_bank, h3_bank = (bank[0], bank[2]), (bank[1], bank[3])
        y_bank, sa_bank, ba_bank = (bank[4], bank[5]), bank[6], bank[7]

        @block.sync
        def _(sp):
            x_rows = x.rearrange("b (h p) d -> (b h) p d", p=P)
            side_rows = side.rearrange("b (h p) d -> (b h) p d", p=P)
            t_seqs = t_scratch.rearrange("(b p) n -> b p n", p=P)
            out_rows = out.rearrange("b (h p) d -> (b h) p d", p=P)

            def load(g, c, ring_full=True):
                slot, i = c % RING, seq(g, c)
                if ring_full:
                    sp.wait_ge(value_lo_ready, i - RING + 1)
                sp.dma_start(x_in[slot][:, :, :], x_rows[bass.ds(SC * i, SC)].rearrange("k p d -> p k d")
                             ).then_inc(seq_loaded[slot], 16)
                sp.dma_start(kv[slot][:, :, :], side_rows[bass.ds(SC * i, SC)].rearrange("k p d -> p k d")
                             ).then_inc(seq_loaded[slot], 16)

            def store(g, c):
                sp.wait_ge(oT_copied, seq(g, c) + 1)
                sp.dma_start(t_scratch[bass.ds(P * seq(g, c), P), :], oT[c % 2][:, :]
                             ).then_inc(t_stored[c % 2], 16)

            def store_rows(r):
                sp.wait_ge(rows_copied, r + 1)
                cols = bass.ds(GCOLS * r, GCOLS)
                sp.dma_start(hot_scratch[:, :, cols].rearrange("w e c n -> (w e) c n"), hot_rows[:, :]
                             ).then_inc(rows_stored, 16)
                sp.dma_start(scale_scratch[:, cols], scale_rows[:, :]).then_inc(rows_stored, 16)

            def step(g, c):
                if not isinstance(g, int) or c + 3 < BATCH:
                    load(g, c + 3)
                store(g, c - 1)
                if c % GROUP == 3 and c >= 11:
                    store_rows(group_of(g, c, 11))

            load(0, 0, ring_full=False)
            sp.dma_start(gate_in[:, :], gate_w).then_inc(small_loaded, 16)
            sp.dma_start(nw[:, :], norm_w.rearrange("(c p) -> p c", p=P),
                         allow_slow_non_contiguous=True).then_inc(small_loaded, 16)
            sp.dma_start(embed_in[:, :], embed).then_inc(small_loaded, 16)
            sp.dma_start(itok_in[:, :], itok.partition_broadcast(STAGES)).then_inc(small_loaded, 16)
            for c in range(1, RING):
                load(0, c, ring_full=False)
            for c in HEAD[1:]:
                step(0, c)
            with sp.Fori(0, LOOPS) as g:
                for c in LOOP:
                    step(g, c)

            def load_tile(g, c, buffers_used=True):
                par, cols = c % 2, bass.ds(KT * tile_no(g, c), KT)
                if buffers_used:
                    sp.wait_ge(z_lo_ready, tile_no(g, c) - 1)
                sp.dma_start(t_in[par][:, :, :, :].rearrange("p b c s -> p b (c s)"),
                             t_seqs[bass.ds(2 * tile_no(g, c), 2)].rearrange("b p n -> p b n")
                             ).then_inc(tile_loaded[par], 16)
                for w, dst in enumerate((mask1, mask_d)):
                    rows = hot_scratch[w, :, cols].rearrange("e k n -> e (k n)").unsqueeze(1)
                    sp.dma_start(dst[par][:, :], rows.to_broadcast([E, R, TILE])).then_inc(tile_loaded[par], 16)
                for w, dst in enumerate((rho, rstd)):
                    row = scale_scratch[w, cols].rearrange("k n -> (k n)")
                    sp.dma_start(dst[par][:, :], row.partition_broadcast(P)).then_inc(tile_loaded[par], 16)

            def load_x(g, c):
                sp.dma_start(x_out[c % 2][:, :, :],
                             x_rows[bass.ds(KT * tile_no(g, c), KT)].rearrange("k p d -> p k d")
                             ).then_inc(x_loaded[c % 2], 16)

            def store_out(g, c):
                half = KT // 2
                for ready, k in ((out_a_ready, 0), (out_b_ready, half)):
                    sp.wait_ge(ready, tile_no(g, c) + 1)
                    sp.dma_start(out_rows[bass.ds(KT * tile_no(g, c) + k, half)].rearrange("k p d -> p k d"),
                                 x_out[c % 2][:, k:k + half, :]).then_inc(out_stored[c % 2], 16)

            def stored(g, c):
                sp.wait_ge(out_stored[c % 2], 32 * (g + c // 2 + 1))

            sp.wait_ge(wT_ready, JOBS)
            for k in range(2):
                sp.wait_ge(t_stored[k], 32)
            sp.wait_ge(rows_stored, 32)
            load_tile(0, 0, buffers_used=False)
            load_tile(0, 1, buffers_used=False)
            for c in TAIL:
                step(0, c)
            store(0, BATCH - 1)
            for k in range(2):
                sp.wait_ge(t_stored[k], 16 * BATCH // 2)
            sp.wait_ge(gate_ready, BATCH)
            load_x(0, 0)
            load_x(0, 1)
            store_rows(6)
            store_rows(7)
            sp.wait_ge(rows_stored, 32 * BATCH // GROUP)
            with sp.Fori(0, 7) as g:
                for c in (1, 2):
                    load_tile(g, c + 1)
                    store_out(g, c - 1)
                    stored(g, c - 1)
                    load_x(g, c + 1)
            store_out(0, TILES - 2)
            store_out(0, TILES - 1)
            stored(0, TILES - 2)
            stored(0, TILES - 1)

        @block.gpsimd
        def _(pool):
            nc.gpsimd.memset(ident[:, :], 0.0).then_inc(const_ready, 1)
            pool.wait_ge(const_ready, 1)
            nc.gpsimd.affine_select(out=ident[:, :], in_=ident[:, :], compare_op=ALU.not_equal, fill=1.0,
                                    base=0, pattern=[[-1, P]], channel_multiplier=1).then_inc(const_ready, 1)
            nc.gpsimd.memset(ones[:, :], 1.0).then_inc(const_ready, 1)
            nc.gpsimd.iota(rank_key[:, :], pattern=[[-1, E]], base=E, channel_multiplier=0,
                           allow_small_or_imprecise_dtypes=True).then_inc(const_ready, 1)
            nc.gpsimd.iota(stage_id[:, :], pattern=[[0, 1]], base=0, channel_multiplier=1,
                           allow_small_or_imprecise_dtypes=True).then_inc(const_ready, 1)

            def value_low(g, c):
                pool.wait_ge(value_hi_ready, seq(g, c) + 1)
                hi, lo = value[c % 2]
                nc.gpsimd.tensor_tensor(lo[:, :, :], kv[c % RING][:, :, :], f32(hi[:, :, :]), ALU.subtract
                                        ).then_inc(value_lo_ready, 1)

            def sum_squares(g, c):
                pool.wait_ge(oT_squared, seq(g, c) + 1)
                nc.gpsimd.tensor_tensor(sq_sum[c % 2][:, :], oT_sq[c % 2][:, 0:S], oT_sq[c % 2][:, S:2 * S], ALU.add
                                        ).then_inc(sq_summed, 1)

            def step(g, c):
                value_low(g, c)
                if c >= 1:
                    sum_squares(g, c - 1)

            for c in HEAD:
                if c == JOB_STEPS[0]:
                    pool.wait_ge(w_loaded, 16 * W_LOADS)
                    for src, dst in ((b1_in, b1_by_j), (b3_in, b3_by_j)):
                        nc.gpsimd.tensor_copy(dst[:, :, :, :].rearrange("p j e r -> p e j r"),
                                              src[:, :, :].rearrange("p e (j r) -> p e j r", j=FC)
                                              ).then_inc(b_ordered, 1)
                step(0, c)
            with pool.Fori(0, LOOPS) as g:
                for c in LOOP:
                    step(g, c)
            for c in TAIL:
                step(0, c)

            def t_low(g, c):
                pool.wait_ge(t_hi_ready, tile_no(g, c) + 1)
                nc.gpsimd.tensor_tensor(t_lo[c % 2][:, :, :], t_scaled[:, :, :], f32(t_hi[c % 2][:, :, :]),
                                        ALU.subtract).then_inc(t_lo_ready, 1)

            def v_low(g, c, k):
                pool.wait_ge(v_hi_ready, 4 * tile_no(g, c) + k + 1)
                nc.gpsimd.tensor_tensor(v_lo[k][:, :], v_full[k][:, :], f32(v_hi[k][:, :]),
                                        ALU.subtract).then_inc(v_lo_ready, 1)

            def add_residual(g, c):
                half = x_out[c % 2][:, KT // 2:KT, :]
                pool.wait_ge(y_scaled_ready, tile_no(g, c) + 1)
                pool.wait_ge(x_loaded[c % 2], 16 * (g + c // 2 + 1))
                nc.gpsimd.tensor_tensor(half, y_scaled[:, :, :], half, ALU.add).then_inc(out_b_ready, 1)

            t_low(0, 0)
            v_low(0, 0, 0)
            v_low(0, 0, 1)
            sum_squares(0, BATCH - 1)
            v_low(0, 0, 2)
            v_low(0, 0, 3)
            t_low(0, 1)
            with pool.Fori(0, 7) as g:
                for c in (1, 2):
                    for k in range(4):
                        v_low(g, c, k)
                    add_residual(g, c - 1)
                    t_low(g, c + 1)
            for k in range(4):
                v_low(0, TILES - 1, k)
            add_residual(0, TILES - 2)
            add_residual(0, TILES - 1)

        @block.scalar
        def _(act):
            for dst, src in ((a1_in[:, :], a1.rearrange("e r d -> (e r) d")),
                             (a3_in[:, :], a3.rearrange("e r d -> (e r) d")),
                             (w1_in[:, :, :], w1.rearrange("(p j) d -> p j d", j=FC)),
                             (w3_in[:, :, :], w3.rearrange("(p j) d -> p j d", j=FC)),
                             (b1_in[:, :, :], b1.rearrange("e (p j) r -> p e (j r)", j=FC)),
                             (b3_in[:, :, :], b3.rearrange("e (p j) r -> p e (j r)", j=FC)),
                             (w2_in[:, :, :], w2.rearrange("(c p) f -> p c f", p=P)),
                             (a2_in[:, :], a2.rearrange("e r f -> (e r) f")),
                             (b2_in[:, 0], b2[:, 0:P, :].rearrange("e p r -> p e r")),
                             (b2_in[:, 1], b2[:, P:D, :].rearrange("e p r -> p e r"))):
                act.dma_start(dst, src).then_inc(w_loaded, 16)

            act.wait_ge(gate_wT_ready, 1)
            for c in range(DC):
                last = nc.scalar.activation(gateT[:, c, :], row_bank[:, c * E:(c + 1) * E], ACT.Copy,
                                            scale=nw_at(c))
            last.then_inc(gate_w_copied, 1)

            def weight_high(i, k):
                n = job_no(i, k)
                act.wait_ge(wT_ready, n + 1)
                for col, cols, hi, lo, scale in jobs[n][1]:
                    last = nc.scalar.activation(hi, w_bank[n % 2][:, col:col + cols], ACT.Copy, scale=scale)
                last.then_inc(w_hi_ready, 1)

            def qk_high(g, c):
                act.wait_ge(qkT_ready, seq(g, c) + 1)
                nc.scalar.activation(qT[c % 2][0][:, :], qT_bank[:, :], ACT.Copy).then_inc(qT_hi_ready, 1)
                nc.scalar.activation(kT[c % 2][0][:, :], kT_bank[:, :], ACT.Copy).then_inc(kT_hi_ready, 1)

            def value_high(g, c):
                act.wait_ge(seq_loaded[c % RING], 32 * (g + c // RING + 1))
                nc.scalar.activation(value[c % 2][0][:, :, :], kv[c % RING][:, :, :], ACT.Copy
                                     ).then_inc(value_hi_ready, 1)

            def exp(g, c):
                act.wait_ge(max_ready, seq(g, c) + 1)
                for h in range(SC):
                    last = nc.scalar.activation(prob[c % 2][:, h, :], score_bank[:, h * S:(h + 1) * S], ACT.Exp,
                                                bias=neg_max[c % 2][:, h:h + 1],
                                                accum_out=row_sum[c % RING][:, h:h + 1])
                last.then_inc(prob_ready, 1)

            def probT_high(g, c):
                act.wait_ge(probT_ready, seq(g, c) + 1)
                nc.scalar.activation(probT[c % 2][0][:, :], probT_bank[:, :], ACT.Copy).then_inc(probT_hi_ready, 1)

            def copy_oT(g, c):
                act.wait_ge(o_ready, seq(g, c) + 1)
                if c >= 2:
                    act.wait_ge(t_stored[c % 2], 16 * (2 * g + c // 2))
                nc.scalar.activation(oT[c % 2][:, :], o_bank[:, :], ACT.Copy).then_inc(oT_copied, 1)
                nc.scalar.activation(oT_sq[c % 2][:, :], o_bank[:, :], ACT.Square).then_inc(oT_squared, 1)

            def exp_gap(r):
                act.wait_ge(gap_ready, r + 1)
                nc.scalar.activation(scales[:, 0, :], g_t[:, :], ACT.Exp).then_inc(rho_ready, 1)

            def copy_rows(r, src, first=False):
                act.wait_ge(rows_ready, r + 1)
                if not first:
                    act.wait_ge(rows_stored, 32 * r)
                nc.scalar.activation(hot_rows[:, :], src[:, 0:P], ACT.Copy)
                nc.scalar.activation(scale_rows[:, :], src[0:2 * GCOLS, P:2 * P], ACT.Copy).then_inc(rows_copied, 1)

            def step(g, c, jobs_here=False):
                exp(g, c)
                if jobs_here:
                    weight_high(c, 0)
                if not isinstance(g, int) or c + 1 < BATCH:
                    qk_high(g, c + 1)
                if jobs_here:
                    weight_high(c, 1)
                value_high(g, c)
                if jobs_here:
                    weight_high(c, 2)
                if c >= 1:
                    copy_oT(g, c - 1)
                if jobs_here:
                    weight_high(c, 3)
                probT_high(g, c)
                if jobs_here:
                    weight_high(c, 4)
                if c % GROUP == 1 and c >= 9:
                    exp_gap(group_of(g, c, 9))
                if c % GROUP == 2 and c >= 10:
                    copy_rows(group_of(g, c, 10), row_bank, first=isinstance(g, int) and c == 10)

            qk_high(0, 0)
            for c in HEAD:
                step(0, c, c in JOB_STEPS)
            with act.Fori(0, LOOPS) as g:
                for c in LOOP:
                    step(g, c)
            def t_high(g, c):
                act.wait_ge(t_scaled_ready, tile_no(g, c) + 1)
                nc.scalar.activation(t_hi[c % 2][:, :, :], t_scaled[:, :, :], ACT.Copy).then_inc(t_hi_ready, 1)

            def v_high(g, c, k):
                act.wait_ge(v_ready, 4 * tile_no(g, c) + k + 1)
                nc.scalar.activation(v_hi[k][:, :], v_full[k][:, :], ACT.Copy).then_inc(v_hi_ready, 1)

            def first_silu(g, c, j):
                act.wait_ge(h1_first, chunk_no(g, c, j) + 1)
                nc.scalar.activation(silu_a[j % 2][:, :], h1_bank[j % 2][:, :], ACT.Silu).then_inc(silu_a_ready, 1)

            def second_silu(g, c, j):
                act.wait_ge(h1_second, chunk_no(g, c, j) + 1)
                nc.scalar.activation(silu_b[:, :], h1_bank[j % 2][:, :], ACT.Silu).then_inc(silu_b_ready, 1)

            def down_high(g, c, j, buffer_used=True):
                n = chunk_no(g, c, j)
                if buffer_used:
                    act.wait_ge(down_done, n - 1)
                act.wait_ge(act_s_ready, n + 1)
                nc.scalar.activation(s_hi[j % 2][:, :], act_s[j % 2][:, :], ACT.Copy).then_inc(s_hi_ready, 1)
                act.wait_ge(act_br_ready, n + 1)
                nc.scalar.activation(br_hi[j % 2][:, :], act_br[j % 2][:, :], ACT.Copy).then_inc(br_hi_ready, 1)

            def z_high(g, c):
                act.wait_ge(z_ready, tile_no(g, c) + 1)
                nc.scalar.activation(z_hi[:, :], z_a[:, :], ACT.Copy).then_inc(z_hi_ready, 1)

            def copy_y0(g, c):
                act.wait_ge(y_ready, tile_no(g, c) + 1)
                nc.scalar.activation(yT[:, 0, :], y_bank[0][:, :], ACT.Copy).then_inc(y0_copied, 1)

            def scale_y(g, c):
                act.wait_ge(yT_ready, 2 * tile_no(g, c) + 1)
                act.wait_ge(rt_ready, tile_no(g, c) + 1)
                for k in range(KT // 2, KT):
                    last = nc.scalar.activation(y_scaled[:, k - KT // 2, :], h3_bank[0][:, (k % 2) * D:(k % 2 + 1) * D],
                                                ACT.Copy, scale=rt[c % 2][:, k:k + 1])
                last.then_inc(y_scaled_ready, 1)

            def act_tile(g, c, first=False, last=False):
                v_high(g, c, 0)
                v_high(g, c, 1)
                if first:
                    copy_oT(0, BATCH - 1)
                else:
                    second_silu(g, c - 1, FC - 1)
                    act.wait_ge(h3_second, chunk_no(g, c))
                v_high(g, c, 2)
                v_high(g, c, 3)
                if first:
                    exp_gap(6)
                    copy_rows(6, row_bank)
                else:
                    down_high(g, c - 1, FC - 1)
                first_silu(g, c, 0)
                if not first:
                    z_high(g, c - 1)
                for j in range(1, FC):
                    first_silu(g, c, j)
                    if j == 2 and not first:
                        copy_y0(g, c - 1)
                    second_silu(g, c, j - 1)
                    if j == 3 and first:
                        copy_rows(7, h1_bank[0])
                    if j == 3 and not first:
                        scale_y(g, c - 1)
                    down_high(g, c, j - 1, buffer_used=not (first and j < 3))
                    if j == 2 and first:
                        exp_gap(7)
                    if j == 6 and not last:
                        t_high(g, c + 1)

            for c in TAIL:
                step(0, c)
                if c == BATCH - 2:
                    t_high(0, 0)
            act_tile(0, 0, first=True)
            with act.Fori(0, 7) as g:
                for c in (1, 2):
                    act_tile(g, c)
            end = TILES - 1
            act_tile(0, end, last=True)
            second_silu(0, end, FC - 1)
            down_high(0, end, FC - 1)
            z_high(0, end)
            copy_y0(0, end)
            act.wait_ge(out_b_ready, end)
            scale_y(0, end)

        @block.vector
        def _(dve):
            dve.wait_ge(small_loaded, 16 * SMALL_LOADS)
            dve.wait_ge(const_ready, 5)
            nc.vector.tensor_copy(itok_f[:, :], itok_in[:, :]).then_inc(stage_ready, 1)
            dve.wait_ge(stage_ready, 1)
            nc.vector.tensor_scalar(stage_hot[:, :], itok_f[:, :], stage_id[:, 0:1], None, ALU.is_equal
                                    ).then_inc(stage_ready, 1)
            dve.wait_ge(bias_ready, 1)
            nc.vector.tensor_copy(bias[:, :, :].rearrange("p h b -> p (h b)"), bias_bank[:, 0:SC * BATCH]
                                  ).then_inc(bias_copied, 1)
            dve.wait_ge(bias_copied, 1)

            def weight_low(i, k):
                n = job_no(i, k)
                dve.wait_ge(w_hi_ready, n + 1)
                for col, cols, hi, lo, scale in jobs[n][1]:
                    last = nc.vector.scalar_tensor_tensor(lo, w_bank[n % 2][:, col:col + cols], scale, f32(hi),
                                                          ALU.mult, ALU.subtract)
                last.then_inc(w_lo_ready, 1)

            def add_bias(g, c, buffer_used=True):
                if buffer_used:
                    dve.wait_ge(qkT_ready, seq(g, c) - 1)
                dve.wait_ge(seq_loaded[c % RING], 32 * (g + c // RING + 1))
                for h in range(SC):
                    last = nc.vector.tensor_scalar(q[c % 2][:, h, :], x_in[c % RING][:, h, :],
                                                   bias[:, h, bass.ds(seq(g, c), 1)], None, ALU.add)
                last.then_inc(q_ready, 1)

            def qk_low(g, c):
                dve.wait_ge(qT_hi_ready, seq(g, c) + 1)
                nc.vector.tensor_tensor(qT[c % 2][1][:, :], qT_bank[:, :], f32(qT[c % 2][0][:, :]), ALU.subtract)
                dve.wait_ge(kT_hi_ready, seq(g, c) + 1)
                nc.vector.tensor_tensor(kT[c % 2][1][:, :], kT_bank[:, :], f32(kT[c % 2][0][:, :]), ALU.subtract
                                        ).then_inc(qkT_lo_ready, 1)

            def row_max(g, c):
                dve.wait_ge(scores_ready, seq(g, c) + 1)
                nc.vector.tensor_reduce(neg_max[c % 2][:, :], score_bank[:, :].rearrange("p (h t) -> p h t", h=SC),
                                        AXIS.X, ALU.max, negate=True).then_inc(max_ready, 1)

            def probT_low(g, c):
                dve.wait_ge(probT_hi_ready, seq(g, c) + 1)
                nc.vector.tensor_tensor(probT[c % 2][1][:, :], probT_bank[:, :], f32(probT[c % 2][0][:, :]),
                                        ALU.subtract).then_inc(probT_lo_ready, 1)

            def keep_gate(g, c):
                dve.wait_ge(gate_ready, seq(g, c) + 1)
                r = row_sum[c % RING]
                col = SC * (c % GROUP)
                nc.vector.scalar_tensor_tensor(eps_r2[:, :], r[:, :], EPS, r[:, :], ALU.mult, ALU.mult
                                               ).then_inc(eps_ready, 1)
                dve.wait_ge(eps_ready, seq(g, c) + 1)
                halves = gate_bank[:, 0:SC * GATE_STRIDE].rearrange("p (h n) -> p h n", h=SC)
                nc.vector.scalar_tensor_tensor(mean_sq[:, col:col + SC], halves[:, :, E], 1.0 / D,
                                               eps_r2[:, :], ALU.mult, ALU.add)
                nc.vector.tensor_scalar(logits[:, col:col + SC, :], halves[:, :, 0:E], 1.0, None,
                                        ALU.mult).then_inc(gate_read, 1)

            ROUTE_OPS = 30

            def link(r, k, ins):
                ins.then_inc(route_chain, 1)
                dve.wait_ge(route_chain, ROUTE_OPS * r + k)

            def bcast(ap):
                return ap.unsqueeze(2).to_broadcast([P, GCOLS, E])

            rank = rank_key[:, :].unsqueeze(1).to_broadcast([P, GCOLS, E])

            def pick(r, k, best, hot):
                link(r, k, nc.vector.tensor_reduce(best[:, :], g_logits[:, :, :], AXIS.X, ALU.max))
                link(r, k + 1, nc.vector.tensor_tensor(g_key[:, :, :], g_logits[:, :, :], bcast(best[:, :]), ALU.is_equal))
                link(r, k + 2, nc.vector.tensor_tensor(g_key[:, :, :], g_key[:, :, :], rank, ALU.mult))
                link(r, k + 3, nc.vector.tensor_reduce(g_best[:, :], g_key[:, :, :], AXIS.X, ALU.max))
                link(r, k + 4, nc.vector.tensor_tensor(hot[:, :, :], g_key[:, :, :], bcast(g_best[:, :]), ALU.is_equal))

            def route_first(g, c):
                r = group_of(g, c, 6)
                dve.wait_ge(gate_read, GROUP * r + GROUP)
                link(r, 1, nc.vector.tensor_copy(g_logits[:, :, :], logits[:, :, :]))
                link(r, 2, nc.vector.tensor_copy(g_z[:, :], mean_sq[:, :]))
                pick(r, 3, g_top1, g_hot1)

            def route_second(g, c, first=False):
                r = group_of(g, c, 7)
                link(r, 8, nc.vector.scalar_tensor_tensor(g_logits[:, :, :], g_hot1[:, :, :], -3.0e38,
                                                          g_logits[:, :, :], ALU.mult, ALU.add))
                pick(r, 9, g_top2, g_hot2)
                if not first:
                    dve.wait_ge(rows_ready, r)
                link(r, 14, nc.vector.tensor_copy(hots[:, 0].rearrange("p e c -> p c e"), g_hot1[:, :, :]))
                link(r, 15, nc.vector.tensor_tensor(hots[:, 1].rearrange("p e c -> p c e"), g_hot2[:, :, :], g_hot1[:, :, :], ALU.subtract))

            def route_rstd(g, c):
                r = group_of(g, c, 8)
                y_bits, z_bits = g_y[:, :].bitcast(I32), g_z[:, :].bitcast(I32)
                link(r, 16, nc.vector.tensor_scalar(y_bits, z_bits, 1, None, ALU.logical_shift_right))
                link(r, 17, nc.vector.tensor_scalar(y_bits, y_bits, -1.0, RSQRT_SEED, ALU.mult, ALU.add))
                for n in range(3):
                    target = scales[:, 1] if n == 2 else g_y[:, :]
                    link(r, 18 + 3 * n, nc.vector.tensor_tensor(g_t[:, :], g_y[:, :], g_y[:, :], ALU.mult))
                    link(r, 19 + 3 * n, nc.vector.scalar_tensor_tensor(g_t[:, :], g_t[:, :], -0.5, g_z[:, :],
                                                                       ALU.mult, ALU.mult))
                    link(r, 20 + 3 * n, nc.vector.scalar_tensor_tensor(target, g_t[:, :], 1.5, g_y[:, :],
                                                                       ALU.add, ALU.mult))

            def route_gap(g, c):
                r = group_of(g, c, 9)
                link(r, 27, nc.vector.tensor_tensor(g_t[:, :], g_top2[:, :], g_top1[:, :], ALU.subtract))
                nc.vector.tensor_tensor(g_t[:, :], g_t[:, :], scales[:, 1], ALU.mult).then_inc(gap_ready, 1)

            def route_weight(g, c):
                r = group_of(g, c, 10)
                dve.wait_ge(rho_ready, r + 1)
                link(r, 28, nc.vector.tensor_scalar(g_y[:, :], scales[:, 0], 1.0, None, ALU.add))
                link(r, 29, nc.vector.reciprocal(g_y[:, :], g_y[:, :]))
                link(r, 30, nc.vector.tensor_scalar(w_first[:, bass.ds(GCOLS * r, GCOLS)], g_y[:, :], 1.0, None, ALU.mult))

            def route_part(g, c):
                if c % GROUP == 2 and c >= 10:
                    route_weight(g, c)
                if c % GROUP == 2 and c >= 6:
                    route_first(g, c)
                if c % GROUP == 3 and c >= 7:
                    route_second(g, c, first=isinstance(g, int) and c == 7)
                if c % GROUP == 0 and c >= 8:
                    route_rstd(g, c)
                if c % GROUP == 1 and c >= 9:
                    route_gap(g, c)

            def step(g, c, jobs_here=False):
                row_max(g, c)
                if jobs_here:
                    weight_low(c, 0)
                if not isinstance(g, int) or c + 1 < BATCH:
                    qk_low(g, c + 1)
                if jobs_here:
                    weight_low(c, 1)
                route_part(g, c)
                if c >= 2:
                    keep_gate(g, c - 2)
                if jobs_here:
                    weight_low(c, 2)
                if not isinstance(g, int) or c + 2 < BATCH:
                    add_bias(g, c + 2)
                if jobs_here:
                    weight_low(c, 3)
                probT_low(g, c)
                if jobs_here:
                    weight_low(c, 4)

            add_bias(0, 0, buffer_used=False)
            add_bias(0, 1, buffer_used=False)
            qk_low(0, 0)
            for c in HEAD:
                step(0, c, c in JOB_STEPS)
            with dve.Fori(0, LOOPS) as g:
                for c in LOOP:
                    step(g, c)

            def scale_t(g, c, buffer_used=True):
                dve.wait_ge(tile_loaded[c % 2], TILE_LOADS * (g + c // 2 + 1))
                if buffer_used:
                    dve.wait_ge(t_lo_ready, tile_no(g, c))
                for dc in range(DC):
                    last = nc.vector.tensor_tensor(t_scaled[:, dc, :].rearrange("p (b s) -> p b s", b=2),
                                                   t_in[c % 2][:, :, dc, :],
                                                   rstd[c % 2][:, :].rearrange("p (b s) -> p b s", b=2), ALU.mult)
                last.then_inc(t_scaled_ready, 1)

            def load_weight(g, c, buffer_used=True):
                if buffer_used:
                    dve.wait_ge(out_a_ready, tile_no(g, c) - 1)
                    dve.wait_ge(y_scaled_ready, tile_no(g, c) - 1)
                nc.vector.tensor_scalar(rt[c % 2][:, :], w_first[:, bass.ds(KT * tile_no(g, c), KT)], 1.0, None,
                                        ALU.mult).then_inc(rt_ready, 1)

            def mask_u(g, c, first=False):
                dve.wait_ge(u_ready, tile_no(g, c) + 1)
                if first:
                    dve.wait_ge(value_lo_ready, BATCH)
                else:
                    dve.wait_ge(v_lo_ready, 4 * tile_no(g, c))
                for k in range(4):
                    u = (h1_bank[0], h3_bank[0])[k % 2]
                    m = (mask1, mask_d)[k // 2][c % 2]
                    nc.vector.tensor_tensor(v_full[k][:, :], u[:, :], m[:, :], ALU.mult).then_inc(v_ready, 1)

            def first_act(g, c, j):
                dve.wait_ge(h3_first, chunk_no(g, c, j) + 1)
                dve.wait_ge(silu_a_ready, chunk_no(g, c, j) + 1)
                nc.vector.tensor_tensor(act_a[j % 2][:, :], silu_a[j % 2][:, :], h3_bank[j % 2][:, :], ALU.mult
                                        ).then_inc(act_a_ready, 1)

            def second_act(g, c, j):
                n = chunk_no(g, c, j)
                dve.wait_ge(h3_second, n + 1)
                dve.wait_ge(silu_b_ready, n + 1)
                nc.vector.tensor_tensor(act_b[:, :], silu_b[:, :], h3_bank[j % 2][:, :], ALU.mult
                                        ).then_inc(act_b_ready, 1)
                dve.wait_ge(act_b_ready, n + 1)
                nc.vector.tensor_tensor(act_br[j % 2][:, :], act_b[:, :], rho[c % 2][:, :], ALU.mult
                                        ).then_inc(act_br_ready, 1)
                dve.wait_ge(act_br_ready, n + 1)
                dve.wait_ge(act_a_ready, n + 1)
                nc.vector.tensor_tensor(act_s[j % 2][:, :], act_a[j % 2][:, :], act_br[j % 2][:, :], ALU.add
                                        ).then_inc(act_s_ready, 1)

            def down_low(g, c, j):
                n = chunk_no(g, c, j)
                dve.wait_ge(s_hi_ready, n + 1)
                nc.vector.tensor_tensor(s_lo[j % 2][:, :], act_s[j % 2][:, :], f32(s_hi[j % 2][:, :]), ALU.subtract)
                dve.wait_ge(br_hi_ready, n + 1)
                nc.vector.tensor_tensor(br_lo[j % 2][:, :], act_br[j % 2][:, :], f32(br_hi[j % 2][:, :]), ALU.subtract
                                        ).then_inc(down_in_ready, 1)

            def mask_z(g, c):
                n = tile_no(g, c) + 1
                dve.wait_ge(z_in_ready, n)
                nc.vector.tensor_tensor(z_b[:, :], ba_bank[:, :], mask_d[c % 2][:, :], ALU.mult).then_inc(z_b_ready, 1)
                nc.vector.tensor_tensor(z_a[:, :], sa_bank[:, :], mask1[c % 2][:, :], ALU.mult).then_inc(z_a_ready, 1)
                dve.wait_ge(z_b_ready, n)
                dve.wait_ge(z_a_ready, n)
                nc.vector.tensor_tensor(z_a[:, :], z_a[:, :], z_b[:, :], ALU.add).then_inc(z_ready, 1)
                dve.wait_ge(z_hi_ready, n)
                nc.vector.tensor_tensor(z_lo[:, :], z_a[:, :], f32(z_hi[:, :]), ALU.subtract).then_inc(z_lo_ready, 1)

            def copy_y1(g, c):
                dve.wait_ge(y_ready, tile_no(g, c) + 1)
                nc.vector.tensor_copy(yT[:, 1, :], y_bank[1][:, :]).then_inc(y1_copied, 1)

            def add_residual(g, c):
                dve.wait_ge(yT_ready, 2 * tile_no(g, c) + 2)
                dve.wait_ge(x_loaded[c % 2], 16 * (g + c // 2 + 1))
                for k in range(KT // 2):
                    last = nc.vector.scalar_tensor_tensor(x_out[c % 2][:, k, :], h1_bank[0][:, k * D:(k + 1) * D],
                                                          rt[c % 2][:, k:k + 1], x_out[c % 2][:, k, :],
                                                          ALU.mult, ALU.add)
                last.then_inc(out_a_ready, 1)

            def dve_tile(g, c, first=False, last=False):
                mask_u(g, c, first)
                if first:
                    route_gap(0, 33)
                    keep_gate(0, BATCH - 1)
                else:
                    second_act(g, c - 1, FC - 1)
                    down_low(g, c - 1, FC - 1)
                first_act(g, c, 0)
                if not first:
                    mask_z(g, c - 1)
                for j in range(1, FC):
                    first_act(g, c, j)
                    if j == 2 and not first:
                        copy_y1(g, c - 1)
                    second_act(g, c, j - 1)
                    if j == 3 and not first:
                        add_residual(g, c - 1)
                    if j == 5 and not last:
                        scale_t(g, c + 1)
                        load_weight(g, c + 1, buffer_used=not first)
                    down_low(g, c, j - 1)
                    if j == 1 and first:
                        route_weight(0, 34)
                        route_first(0, 34)
                        route_second(0, 35)
                    if j == 2 and first:
                        route_rstd(0, 36)
                        route_gap(0, 37)
                    if j == 4 and first:
                        route_weight(0, 38)
                        for k in range(2):
                            dve.wait_ge(t_stored[k], 16 * BATCH // 2)

            for c in TAIL:
                step(0, c)
                if c == BATCH - 2:
                    scale_t(0, 0, buffer_used=False)
                    load_weight(0, 0, buffer_used=False)
            route_rstd(0, 32)
            keep_gate(0, BATCH - 2)
            dve_tile(0, 0, first=True)
            with dve.Fori(0, 7) as g:
                for c in (1, 2):
                    dve_tile(g, c)
            end = TILES - 1
            dve_tile(0, end, last=True)
            second_act(0, end, FC - 1)
            down_low(0, end, FC - 1)
            mask_z(0, end)
            copy_y1(0, end)
            add_residual(0, end)

        @block.tensor
        def _(pe):
            def product(dst, w, x_parts, start, stop, grouped=True):
                (w_hi, w_lo), (x_hi, x_lo) = w, x_parts
                nc.tensor.matmul(dst, w_hi, x_hi, start=start, stop=False, skip_group_check=not grouped)
                nc.tensor.matmul(dst, w_hi, x_lo, start=False, stop=False, skip_group_check=not grouped)
                return nc.tensor.matmul(dst, w_lo, x_hi, start=False, stop=stop, skip_group_check=not grouped)

            def at(parts, *index):
                return parts[0][index], parts[1][index]

            ALL = slice(None)

            pe.wait_ge(const_ready, 5)
            pe.wait_ge(small_loaded, 16 * SMALL_LOADS)
            pe.wait_ge(stage_ready, 2)
            for h in range(SC):
                last = nc.tensor.matmul(bias_bank[:, h * BATCH:(h + 1) * BATCH], embed_in[:, h * P:(h + 1) * P],
                                        stage_hot[:, :], start=True, stop=True)
            last.then_inc(bias_ready, 1)
            for c in range(DC):
                last = nc.tensor.transpose(row_bank[:, c * E:(c + 1) * E], gate_in[:, c * P:(c + 1) * P],
                                           ident[0:E, 0:E])
            last.then_inc(gate_wT_ready, 1)

            def weight_job(i, k):
                n = job_no(i, k)
                if n == 0:
                    pe.wait_ge(w_loaded, 16 * W_LOADS)
                    pe.wait_ge(gate_w_copied, 1)
                    pe.wait_ge(bias_copied, 1)
                    pe.wait_ge(b_ordered, 2)
                if n >= 2:
                    pe.wait_ge(w_lo_ready, n - 1)
                for col, cols, src, rows in jobs[n][0]:
                    last = nc.tensor.transpose(w_bank[n % 2][0:P, col:col + cols], src, ident[0:rows, 0:rows])
                last.then_inc(wT_ready, 1)

            def transpose_qk(g, c):
                pe.wait_ge(q_ready, seq(g, c) + 1)
                for src, dst in ((q[c % 2], qT_bank), (kv[c % RING], kT_bank)):
                    for dc in range(DC):
                        for h in range(SC):
                            last = nc.tensor.transpose(dst[:, dc * S + h * P:dc * S + (h + 1) * P],
                                                       src[:, h, dc * P:(dc + 1) * P], ident[:, :])
                last.then_inc(qkT_ready, 1)

            def scores(g, c):
                pe.wait_ge(qkT_lo_ready, seq(g, c) + 1)
                for h in range(SC):
                    for dc in range(DC):
                        last = product(score_bank[:, h * S:(h + 1) * S],
                                       at(qT[c % 2], ALL, slice(dc * S + h * P, dc * S + (h + 1) * P)),
                                       at(kT[c % 2], ALL, slice(dc * S, (dc + 1) * S)), dc == 0, dc == DC - 1)
                last.then_inc(scores_ready, 1)

            def transpose_prob(g, c):
                pe.wait_ge(prob_ready, seq(g, c) + 1)
                for tc in range(SC):
                    for h in range(SC):
                        last = nc.tensor.transpose(probT_bank[:, tc * S + h * P:tc * S + (h + 1) * P],
                                                   prob[c % 2][:, h, tc * P:(tc + 1) * P], ident[:, :])
                last.then_inc(probT_ready, 1)

            def attend(g, c):
                pe.wait_ge(value_lo_ready, seq(g, c) + 1)
                pe.wait_ge(probT_lo_ready, seq(g, c) + 1)
                for dc in range(DC):
                    for tc in range(SC):
                        last = product(o_bank[:, dc * S:(dc + 1) * S],
                                       at(value[c % 2], ALL, tc, slice(dc * P, (dc + 1) * P)),
                                       at(probT[c % 2], ALL, slice(tc * S, (tc + 1) * S)), tc == 0, tc == SC - 1)
                last.then_inc(o_ready, 1)

            def gate(g, c, first=False):
                if first:
                    pe.wait_ge(gate_w_copied, 1)
                else:
                    pe.wait_ge(gate_read, seq(g, c))
                pe.wait_ge(oT_copied, seq(g, c) + 1)
                for h in range(SC):
                    for dc in range(DC):
                        nc.tensor.matmul(gate_bank[:, h * GATE_STRIDE:h * GATE_STRIDE + E],
                                         oT[c % 2][:, dc * S + h * P:dc * S + (h + 1) * P],
                                         gateT[:, dc, :], start=(dc == 0), stop=(dc == DC - 1))
                pe.wait_ge(sq_summed, seq(g, c) + 1)
                for h in range(SC):
                    col = h * GATE_STRIDE + E
                    last = nc.tensor.matmul(gate_bank[:, col:col + 1], sq_sum[c % 2][:, h * P:(h + 1) * P],
                                            ones[:, :], start=True, stop=True)
                last.then_inc(gate_ready, 1)

            def transpose_rows(r, dst):
                pe.wait_ge(rho_ready, r + 1)
                nc.tensor.transpose(dst[:, 0:P], hots[:, :, :, :].rearrange("p w e c -> p (w e c)"), ident[:, :])
                nc.tensor.transpose(dst[0:2 * GCOLS, P:2 * P], scales[:, :, :].rearrange("p w c -> p (w c)"),
                                    ident[:, :]).then_inc(rows_ready, 1)

            def step(g, c, jobs_here=False):
                scores(g, c)
                if jobs_here:
                    weight_job(c, 0)
                if not isinstance(g, int) or c + 1 < BATCH:
                    transpose_qk(g, c + 1)
                if jobs_here:
                    weight_job(c, 1)
                if c % GROUP == 2 and c >= 10:
                    r = group_of(g, c, 10)
                    if isinstance(g, int) and c == 10:
                        pe.wait_ge(w_lo_ready, JOBS)
                    else:
                        pe.wait_ge(rows_copied, r)
                    transpose_rows(r, row_bank)
                if c >= 2:
                    gate(g, c - 2, first=isinstance(g, int) and c == 2)
                if jobs_here:
                    weight_job(c, 2)
                if c >= 1:
                    attend(g, c - 1)
                if jobs_here:
                    weight_job(c, 3)
                transpose_prob(g, c)
                if jobs_here:
                    weight_job(c, 4)

            transpose_qk(0, 0)
            for c in HEAD:
                step(0, c, c in JOB_STEPS)
            pe.wait_ge(w_lo_ready, JOBS)
            with pe.Fori(0, LOOPS) as g:
                for c in LOOP:
                    step(g, c)
            for c in TAIL:
                step(0, c)

            def low_rank(g, c):
                pe.wait_ge(t_lo_ready, tile_no(g, c) + 1)
                for w, dst in ((0, h1_bank[0]), (1, h3_bank[0])):
                    for dc in range(DC):
                        last = product(dst[:, :], at(a13T, ALL, dc, w), (t_hi[c % 2][:, dc], t_lo[c % 2][:, dc]),
                                       dc == 0, dc == DC - 1)
                last.then_inc(u_ready, 1)

            def first_expert(g, c, j):
                f = slice(j * P, (j + 1) * P)
                for wT, bT, dst, k, done in ((w1T, b1T, h1_bank[j % 2], 0, h1_first),
                                             (w3T, b3T, h3_bank[j % 2], 1, h3_first)):
                    for dc in range(DC):
                        product(dst[:, :], at(wT, ALL, dc, f), (t_hi[c % 2][:, dc], t_lo[c % 2][:, dc]), dc == 0, False)
                    if j == 0:
                        pe.wait_ge(v_lo_ready, 4 * tile_no(g, c) + k + 1)
                    product(dst[:, :], at(bT, ALL, f), (v_hi[k][:, :], v_lo[k][:, :]), False, True).then_inc(done, 1)

            def second_expert(g, c, j):
                if j == 0:
                    pe.wait_ge(v_lo_ready, 4 * tile_no(g, c) + 4)
                pe.wait_ge(act_a_ready, chunk_no(g, c, j) + 1)
                f = slice(j * P, (j + 1) * P)
                for bT, dst, k, done in ((b1T, h1_bank[j % 2], 2, h1_second), (b3T, h3_bank[j % 2], 3, h3_second)):
                    product(dst[:, :], at(bT, ALL, f), (v_hi[k][:, :], v_lo[k][:, :]), False, True, grouped=False
                            ).then_inc(done, 1)

            def down_y(g, c, j):
                pe.wait_ge(down_in_ready, chunk_no(g, c, j) + 1)
                for half in range(DC):
                    last = product(y_bank[half][:, :], at(w2T, ALL, j, slice(half * P, (half + 1) * P)),
                                   (s_hi[j % 2][:, :], s_lo[j % 2][:, :]), j == 0, False)
                return last

            def down_z(g, c, j):
                pe.wait_ge(down_in_ready, chunk_no(g, c, j) + 1)
                product(sa_bank[:, :], at(a2T, ALL, j), (s_hi[j % 2][:, :], s_lo[j % 2][:, :]), j == 0, j == FC - 1)
                return product(ba_bank[:, :], at(a2T, ALL, j), (br_hi[j % 2][:, :], br_lo[j % 2][:, :]),
                               j == 0, j == FC - 1)

            def finish_y(g, c):
                pe.wait_ge(z_lo_ready, tile_no(g, c) + 1)
                for half in range(DC):
                    last = product(y_bank[half][:, :], at(b2T, ALL, slice(half * P, (half + 1) * P)),
                                   (z_hi[:, :], z_lo[:, :]), False, True)
                last.then_inc(y_ready, 1)

            def transpose_y(g, c):
                for dst, ks in ((h3_bank[0], (2, 3)), (h1_bank[0], (0, 1))):
                    for k in ks:
                        for half in range(DC):
                            col = (k % 2) * D + half * P
                            last = nc.tensor.transpose(dst[:, col:col + P], yT[:, half, k * P:(k + 1) * P], ident[:, :])
                    last.then_inc(yT_ready, 1)

            def wait_y_copied(g, c):
                pe.wait_ge(y0_copied, tile_no(g, c) + 1)
                pe.wait_ge(y1_copied, tile_no(g, c) + 1)

            def pe_tile(g, c, first=False, last=False):
                n = chunk_no(g, c)
                if not first:
                    pe.wait_ge(act_b_ready, n - 1)
                low_rank(g, c)
                if first:
                    gate(0, BATCH - 2)
                    attend(0, BATCH - 1)
                else:
                    second_expert(g, c - 1, FC - 1)
                    down_y(g, c - 1, FC - 2)
                    down_z(g, c - 1, FC - 2).then_inc(down_done, 1)
                pe.wait_ge(v_ready, 4 * tile_no(g, c) + 4)
                first_expert(g, c, 0)
                if first:
                    gate(0, BATCH - 1)
                    pe.wait_ge(rows_copied, 6)
                    transpose_rows(6, row_bank)
                else:
                    down_z(g, c - 1, FC - 1).then_inc(z_in_ready, 1)
                for j in range(1, FC):
                    if j == 4 and first:
                        pe.wait_ge(rows_copied, 8)
                    elif j == 4:
                        pe.wait_ge(out_a_ready, tile_no(g, c))
                        pe.wait_ge(y_scaled_ready, tile_no(g, c))
                    elif not (first and j == 1):
                        pe.wait_ge(act_b_ready, n + j - 1)
                    first_expert(g, c, j)
                    if j == 2 and not first:
                        finish_y(g, c - 1)
                    second_expert(g, c, j - 1)
                    if j == 1 and not first:
                        down_y(g, c - 1, FC - 1).then_inc(down_done, 1)
                    if j == 2:
                        if first:
                            pe.wait_ge(gate_read, BATCH)
                            pe.wait_ge(rows_copied, 7)
                        down_z(g, c, 0)
                        if not first:
                            wait_y_copied(g, c - 1)
                        down_y(g, c, 0).then_inc(down_done, 1)
                    elif j == 3:
                        down_y(g, c, 1)
                        pe.wait_ge(act_b_ready, n + 3)
                        if first:
                            transpose_rows(7, h1_bank[0])
                        else:
                            transpose_y(g, c - 1)
                        down_z(g, c, 1).then_inc(down_done, 1)
                    elif j >= 4:
                        down_y(g, c, j - 2)
                        down_z(g, c, j - 2).then_inc(down_done, 1)

            pe_tile(0, 0, first=True)
            with pe.Fori(0, 7) as g:
                for c in (1, 2):
                    pe_tile(g, c)
            end = TILES - 1
            pe_tile(0, end, last=True)
            second_expert(0, end, FC - 1)
            down_y(0, end, FC - 2)
            down_z(0, end, FC - 2).then_inc(down_done, 1)
            down_z(0, end, FC - 1).then_inc(z_in_ready, 1)
            down_y(0, end, FC - 1).then_inc(down_done, 1)
            finish_y(0, end)
            pe.wait_ge(act_b_ready, chunk_no(0, end, FC))
            wait_y_copied(0, end)
            transpose_y(0, end)


_INS = ['x', 'fside_BxSxS_0', 'itok_B_0_5', 'L0_cond_braak_embed', 'L0_ffn_norm_w', 'L0_ffn_w1', 'L0_ffn_w3',
        'L0_ffn_w2', 'L0_ffn_gate_w', 'L0_ffn_a1', 'L0_ffn_b1', 'L0_ffn_a3', 'L0_ffn_b3', 'L0_ffn_a2', 'L0_ffn_b2']


def kernel(**inputs):
    import numpy as np
    import concourse.bacc as bacc
    from concourse.bass_utils import run_bass_kernel_spmd

    nc = bacc.Bacc("TRN2", target_bir_lowering=False, num_devices=1)
    arrays, args = {}, []
    for name in _INS:
        a = np.ascontiguousarray(inputs[name])
        arrays[f"in_{name}"] = a
        args.append(nc.dram_tensor(f"in_{name}", a.shape, mybir.dt.from_np(a.dtype), kind="ExternalInput").ap())
    args.append(nc.dram_tensor("out_0", (BATCH, S, D), F32, kind="ExternalOutput").ap())
    adaln_moe_ffn(nc, *args)
    r = run_bass_kernel_spmd(nc, [arrays], core_ids=[0])
    return r.results[0]["out_0"]
```

```python
from contextlib import ExitStack

import concourse.bass as bass
from concourse import mybir
from concourse.alu_op_type import AluOpType as ALU

F32 = mybir.dt.float32
F32R = mybir.dt.float32r
BF16 = mybir.dt.bfloat16
I32 = mybir.dt.int32
ACT = mybir.ActivationFunctionType
AXIS = mybir.AxisListType

P = 128
BATCH, S, D = 32, 256, 256
F, E, R = 1024, 8, 16
STAGES = 6
ER = E * R
SC = S // P
DC = D // P
FC = F // P
TILE = 512
KT = TILE // P
TILES = BATCH * S // TILE
COLS = BATCH * SC
SCALING = 32.0 / 16.0
EPS = 1e-06
RING = 4
GROUP = 4
GCOLS = GROUP * SC
RSQRT_SEED = float(0x5F3759DF)


def adaln_moe_ffn(nc, x, side, itok, embed, norm_w, w1, w3, w2, gate_w, a1, b1, a3, b3, a2, b2, out):
    ctx = ExitStack()
    with ctx:
        def sem(name):
            return ctx.enter_context(nc.semaphore(name))

        def sems(name, n):
            return [sem(f"{name}{k}") for k in range(n)]

        def sb(stack, name, shape, dt=F32):
            return stack.enter_context(nc.sbuf_tensor(name, shape, dt))

        bank = [ctx.enter_context(nc.psum_tensor(f"bank{k}", [P, 512], F32)) for k in range(8)]
        t_scratch = nc.dram_tensor("t_scratch", [BATCH * P, DC * S], F32, kind="Internal").ap()
        hot_scratch = nc.dram_tensor("hot_scratch", [2, E, COLS, P], BF16, kind="Internal").ap()
        scale_scratch = nc.dram_tensor("scale_scratch", [2, COLS, P], F32, kind="Internal").ap()

        ident = sb(ctx, "ident", [P, P])
        ones = sb(ctx, "ones", [P, 1])
        rank_key = sb(ctx, "rank_key", [P, E])
        stage_id = sb(ctx, "stage_id", [STAGES, 1])

        def split(name, shape, stack=ctx):
            return sb(stack, name + "_hi", shape, F32R), sb(stack, name + "_lo", shape, F32R)

        w1T = split("w1T", [P, DC, F])
        w3T = split("w3T", [P, DC, F])
        w2T = split("w2T", [P, FC, D])
        a2T = split("a2T", [P, FC, ER])
        a13T = split("a13T", [P, DC, 2, ER])
        b1T = split("b1T", [ER, F])
        b3T = split("b3T", [ER, F])
        b2T = split("b2T", [ER, D])
        gateT = sb(ctx, "gateT", [P, DC, E])
        w_first = sb(ctx, "w_first", [P, COLS])
        logits = sb(ctx, "logits", [P, COLS, E])
        mean_sq = sb(ctx, "mean_sq", [P, COLS])
        row_sum = [sb(ctx, f"row_sum{k}", [P, SC]) for k in range(RING)]
        eps_r2 = sb(ctx, "eps_r2", [P, SC])
        g_logits = sb(ctx, "g_logits", [P, GCOLS, E])
        g_z = sb(ctx, "g_z", [P, GCOLS])
        g_top1 = sb(ctx, "g_top1", [P, GCOLS])
        g_top2 = sb(ctx, "g_top2", [P, GCOLS])
        g_best = sb(ctx, "g_best", [P, GCOLS])
        g_key = sb(ctx, "g_key", [P, GCOLS, E])
        g_hot1 = sb(ctx, "g_hot1", [P, GCOLS, E])
        g_hot2 = sb(ctx, "g_hot2", [P, GCOLS, E])
        g_y = sb(ctx, "g_y", [P, GCOLS])
        g_t = sb(ctx, "g_t", [P, GCOLS])
        hots = sb(ctx, "hots", [P, 2, E, GCOLS])
        scales = sb(ctx, "scales", [P, 2, GCOLS])
        hot_rows = sb(ctx, "hot_rows", [2 * GCOLS * E, P], BF16)
        scale_rows = sb(ctx, "scale_rows", [2 * GCOLS, P])
        gate_in = sb(ctx, "gate_in", [E, D])
        nw = sb(ctx, "nw", [P, DC])
        bias = sb(ctx, "bias", [P, SC, BATCH])
        neg_max = [sb(ctx, f"neg_max{k}", [P, SC]) for k in range(2)]

        early = ExitStack()
        w1_in = sb(early, "w1_in", [P, FC, D])
        w3_in = sb(early, "w3_in", [P, FC, D])
        w2_in = sb(early, "w2_in", [P, DC, F])
        b1_in = sb(early, "b1_in", [P, E, FC * R])
        b3_in = sb(early, "b3_in", [P, E, FC * R])
        b1_by_j = sb(early, "b1_by_j", [P, FC, E, R])
        b3_by_j = sb(early, "b3_by_j", [P, FC, E, R])
        a1_in = sb(early, "a1_in", [ER, D])
        a3_in = sb(early, "a3_in", [ER, D])
        a2_in = sb(early, "a2_in", [ER, F])
        b2_in = sb(early, "b2_in", [P, DC, E, R])
        x_in = [sb(early, f"x_in{k}", [P, SC, D]) for k in range(RING)]
        kv = [sb(early, f"kv{k}", [P, SC, D]) for k in range(RING)]
        q = [sb(early, f"q{k}", [P, SC, D]) for k in range(2)]
        qT = [split(f"qT{k}", [P, DC * S], early) for k in range(2)]
        kT = [split(f"kT{k}", [P, DC * S], early) for k in range(2)]
        prob = [sb(early, f"prob{k}", [P, SC, S]) for k in range(2)]
        value = [split(f"value{k}", [P, SC, D], early) for k in range(2)]
        probT = [split(f"probT{k}", [P, SC * S], early) for k in range(2)]
        oT = [sb(early, f"oT{k}", [P, DC * S]) for k in range(2)]
        oT_sq = [sb(early, f"oT_sq{k}", [P, DC * S]) for k in range(2)]
        sq_sum = [sb(early, f"sq_sum{k}", [P, S]) for k in range(2)]
        embed_in = sb(early, "embed_in", [STAGES, S])
        itok_in = sb(early, "itok_in", [STAGES, BATCH], I32)
        itok_f = sb(early, "itok_f", [STAGES, BATCH])
        stage_hot = sb(early, "stage_hot", [STAGES, BATCH])
        early.close()

        late = ctx
        t_in = [sb(late, f"t_in{k}", [P, 2, DC, S]) for k in range(2)]
        t_scaled = sb(late, "t_scaled", [P, DC, TILE])
        t_hi = [sb(late, f"t_hi{k}", [P, DC, TILE], F32R) for k in range(2)]
        t_lo = [sb(late, f"t_lo{k}", [P, DC, TILE], F32R) for k in range(2)]
        mask1 = [sb(late, f"mask1_{k}", [ER, TILE], BF16) for k in range(2)]
        mask_d = [sb(late, f"mask_d{k}", [ER, TILE], BF16) for k in range(2)]
        rho = [sb(late, f"rho{k}", [P, TILE]) for k in range(2)]
        rstd = [sb(late, f"rstd{k}", [P, TILE]) for k in range(2)]
        v_full = [sb(late, f"v_full{k}", [ER, TILE]) for k in range(4)]
        v_hi = [sb(late, f"v_hi{k}", [ER, TILE], F32R) for k in range(4)]
        v_lo = [sb(late, f"v_lo{k}", [ER, TILE], F32R) for k in range(4)]
        silu_a = [sb(late, f"silu_a{k}", [P, TILE]) for k in range(2)]
        silu_b = sb(late, "silu_b", [P, TILE])
        act_a = [sb(late, f"act_a{k}", [P, TILE]) for k in range(2)]
        act_b = sb(late, "act_b", [P, TILE])
        act_br = [sb(late, f"act_br{k}", [P, TILE]) for k in range(2)]
        act_s = [sb(late, f"act_s{k}", [P, TILE]) for k in range(2)]
        s_hi = [sb(late, f"s_hi{k}", [P, TILE], F32R) for k in range(2)]
        s_lo = [sb(late, f"s_lo{k}", [P, TILE], F32R) for k in range(2)]
        br_hi = [sb(late, f"br_hi{k}", [P, TILE], F32R) for k in range(2)]
        br_lo = [sb(late, f"br_lo{k}", [P, TILE], F32R) for k in range(2)]
        z_a = sb(late, "z_a", [ER, TILE])
        z_b = sb(late, "z_b", [ER, TILE])
        z_hi = sb(late, "z_hi", [ER, TILE], F32R)
        z_lo = sb(late, "z_lo", [ER, TILE], F32R)
        yT = sb(late, "yT", [P, DC, TILE])
        y_scaled = sb(late, "y_scaled", [P, KT // 2, D])
        rt = [sb(late, f"rt{k}", [P, KT]) for k in range(2)]
        x_out = [sb(late, f"x_out{k}", [P, KT, D]) for k in range(2)]

        const_ready = sem("const_ready")
        stage_loaded = sem("stage_loaded")
        gate_loaded = sem("gate_loaded")
        w_loaded = sem("w_loaded")
        b_loaded = sem("b_loaded")
        stage_ready = sem("stage_ready")
        gate_wT_ready = sem("gate_wT_ready")
        gate_w_copied = sem("gate_w_copied")
        b_ordered = sem("b_ordered")
        wT_ready = sem("wT_ready")
        w_hi_ready = sem("w_hi_ready")
        w_lo_ready = sem("w_lo_ready")
        bias_ready = sem("bias_ready")
        bias_copied = sem("bias_copied")
        seq_loaded = sems("seq_loaded", RING)
        q_ready = sem("q_ready")
        qkT_ready = sem("qkT_ready")
        qT_hi_ready = sem("qT_hi_ready")
        kT_hi_ready = sem("kT_hi_ready")
        qkT_lo_ready = sem("qkT_lo_ready")
        scores_ready = sem("scores_ready")
        max_ready = sem("max_ready")
        prob_ready = sem("prob_ready")
        value_hi_ready = sem("value_hi_ready")
        value_lo_ready = sem("value_lo_ready")
        probT_ready = sem("probT_ready")
        probT_hi_ready = sem("probT_hi_ready")
        probT_lo_ready = sem("probT_lo_ready")
        o_ready = sem("o_ready")
        oT_copied = sem("oT_copied")
        oT_squared = sem("oT_squared")
        sq_summed = sem("sq_summed")
        gate_ready = sem("gate_ready")
        eps_ready = sem("eps_ready")
        gate_read = sem("gate_read")
        t_stored = sems("t_stored", 2)
        route_chain = sem("route_chain")
        gap_ready = sem("gap_ready")
        rho_ready = sem("rho_ready")
        rows_ready = sem("rows_ready")
        rows_copied = sem("rows_copied")
        rows_stored = sem("rows_stored")

        tile_loaded = sems("tile_loaded", 2)
        x_loaded = sems("x_loaded", 2)
        out_stored = sems("out_stored", 2)
        rt_ready = sem("rt_ready")
        t_scaled_ready = sem("t_scaled_ready")
        t_hi_ready = sem("t_hi_ready")
        t_lo_ready = sem("t_lo_ready")
        u_ready = sem("u_ready")
        v_ready = sem("v_ready")
        v_hi_ready = sem("v_hi_ready")
        v_lo_ready = sem("v_lo_ready")
        h1_first = sem("h1_first")
        h3_first = sem("h3_first")
        h1_second = sem("h1_second")
        h3_second = sem("h3_second")
        silu_a_ready = sem("silu_a_ready")
        silu_b_ready = sem("silu_b_ready")
        act_a_ready = sem("act_a_ready")
        act_b_ready = sem("act_b_ready")
        act_br_ready = sem("act_br_ready")
        act_s_ready = sem("act_s_ready")
        s_hi_ready = sem("s_hi_ready")
        br_hi_ready = sem("br_hi_ready")
        down_in_ready = sem("down_in_ready")
        down_done = sem("down_done")
        z_in_ready = sem("z_in_ready")
        z_a_ready = sem("z_a_ready")
        z_b_ready = sem("z_b_ready")
        z_ready = sem("z_ready")
        z_hi_ready = sem("z_hi_ready")
        z_lo_ready = sem("z_lo_ready")
        y_ready = sem("y_ready")
        y0_copied = sem("y0_copied")
        y1_copied = sem("y1_copied")
        yT_ready = sem("yT_ready")
        y_scaled_ready = sem("y_scaled_ready")
        out_a_ready = sem("out_a_ready")
        out_b_ready = sem("out_b_ready")

        block = ctx.enter_context(nc.Block())

        def f32(ap):
            return ap.bitcast(F32)

        jobs = []

        def nw_at(c):
            return nw[:, c:c + 1]

        a13_in = (a1_in, a3_in)
        jobs.append(([(128 * (2 * c + w), 128, a13_in[w][:, c * P:(c + 1) * P], ER)
                      for c in range(DC) for w in range(2)],
                     [(256 * c, 256, a13T[0][:, c].rearrange("p w e -> p (w e)"),
                       a13T[1][:, c].rearrange("p w e -> p (w e)"), nw_at(c)) for c in range(DC)]))
        for src, dst in ((w1_in, w1T), (w3_in, w3T)):
            for c in range(DC):
                for j0 in range(0, FC, 4):
                    jobs.append(([(128 * k, 128, src[:, j0 + k, c * P:(c + 1) * P], P) for k in range(4)],
                                 [(0, 512, dst[0][:, c, j0 * P:(j0 + 4) * P],
                                   dst[1][:, c, j0 * P:(j0 + 4) * P], nw_at(c))]))
        FIRST_B_JOB = len(jobs)
        for src, dst in ((b1_by_j, b1T), (b3_by_j, b3T)):
            for j0 in range(0, FC, 4):
                jobs.append(([(128 * k, 128, src[:, j0 + k].rearrange("p e r -> p (e r)"), P) for k in range(4)],
                             [(0, 512, dst[0][:, j0 * P:(j0 + 4) * P],
                               dst[1][:, j0 * P:(j0 + 4) * P], SCALING)]))
        for j0 in range(0, FC, 2):
            jobs.append(([(128 * (2 * k + c), 128, w2_in[:, c, j0 + k:F:FC], P)
                          for k in range(2) for c in range(DC)],
                         [(0, 512, w2T[0][:, j0:j0 + 2].rearrange("p j d -> p (j d)"),
                           w2T[1][:, j0:j0 + 2].rearrange("p j d -> p (j d)"), 1.0)]))
        for j0 in range(0, FC, 4):
            jobs.append(([(128 * k, 128, a2_in[:, j0 + k:F:FC], ER) for k in range(4)],
                         [(0, 512, a2T[0][:, j0:j0 + 4].rearrange("p j e -> p (j e)"),
                           a2T[1][:, j0:j0 + 4].rearrange("p j e -> p (j e)"), 1.0)]))
        jobs.append(([(128 * c, 128, b2_in[:, c].rearrange("p e r -> p (e r)"), P) for c in range(DC)],
                     [(0, 256, b2T[0][:, :], b2T[1][:, :], SCALING)]))
        JOBS = len(jobs)
        JOB_STEPS = range(4, 9)
        JOBS_PER_STEP = JOBS // len(JOB_STEPS)
        B_STEPS = range(3, 5)
        ROUTE_STEP = 9
        W_LOADS, B_LOADS, STAGE_LOADS, GATE_LOADS = 8, 2, 2, 2
        TILE_LOADS = 16 * 5

        def job_no(i, k):
            return (i - JOB_STEPS[0]) * JOBS_PER_STEP + k

        qT_bank, kT_bank, score_bank, probT_bank, o_bank, gate_bank, row_bank, bias_bank = bank
        w_bank = bank[6:8]
        GATE_STRIDE = 16

        def seq(g, c):
            return 4 * g + c

        T0_STEP = BATCH - 2
        HEAD, TAIL = range(0, 12), range(28, 32)
        LOOP = range(12, 16)
        LOOPS = (TAIL[0] - LOOP[0]) // 4

        def group_in(g, c):
            return g + c // 2 + 1

        TILE_LOOPS = (TILES - 4) // 2

        def tile_no(g, c):
            return 2 * g + c

        def chunk_no(g, c, j=0):
            return 2 * FC * g + FC * c + j

        h1_bank, h3_bank = (bank[0], bank[2]), (bank[1], bank[3])
        y_bank, sa_bank, ba_bank = (bank[4], bank[5]), bank[6], bank[7]

        @block.sync
        def _(sp):
            x_rows = x.rearrange("b (h p) d -> (b h) p d", p=P)
            side_rows = side.rearrange("b (h p) d -> (b h) p d", p=P)
            t_seqs = t_scratch.rearrange("(b p) n -> b p n", p=P)
            out_rows = out.rearrange("b (h p) d -> (b h) p d", p=P)

            def load(g, c, ring_full=True):
                slot, i = c % RING, seq(g, c)
                if ring_full:
                    sp.wait_ge(value_lo_ready, i - RING + 1)
                sp.dma_start(x_in[slot][:, :, :], x_rows[bass.ds(SC * i, SC)].rearrange("k p d -> p k d")
                             ).then_inc(seq_loaded[slot], 16)
                sp.dma_start(kv[slot][:, :, :], side_rows[bass.ds(SC * i, SC)].rearrange("k p d -> p k d")
                             ).then_inc(seq_loaded[slot], 16)

            def store(g, c):
                sp.wait_ge(oT_copied, seq(g, c) + 1)
                sp.dma_start(t_scratch[bass.ds(P * seq(g, c), P), :], oT[c % 2][:, :]
                             ).then_inc(t_stored[c % 2], 16)

            def store_rows(r):
                sp.wait_ge(rows_copied, r + 1)
                cols = bass.ds(GCOLS * r, GCOLS)
                sp.dma_start(hot_scratch[:, :, cols].rearrange("w e c n -> (w e) c n"), hot_rows[:, :]
                             ).then_inc(rows_stored, 16)
                sp.dma_start(scale_scratch[:, cols], scale_rows[:, :]).then_inc(rows_stored, 16)

            def step(g, c):
                load(g, c + 3)
                store(g, c - 1)

            sp.dma_start(itok_in[:, :], itok.partition_broadcast(STAGES)).then_inc(stage_loaded, 16)
            sp.dma_start(embed_in[:, :], embed).then_inc(stage_loaded, 16)
            load(0, 0, ring_full=False)
            sp.dma_start(gate_in[:, :], gate_w).then_inc(gate_loaded, 16)
            sp.dma_start(nw[:, :], norm_w.rearrange("(c p) -> p c", p=P),
                         allow_slow_non_contiguous=True).then_inc(gate_loaded, 16)
            for c in range(1, RING):
                load(0, c, ring_full=False)
            for c in HEAD[1:]:
                step(0, c)
            with sp.Fori(0, LOOPS) as g:
                for c in LOOP:
                    step(g, c)

            def load_tile(g, c, buffers_used=True):
                par, cols = c % 2, bass.ds(KT * tile_no(g, c), KT)
                if buffers_used:
                    sp.wait_ge(z_lo_ready, tile_no(g, c) - 1)
                sp.dma_start(t_in[par][:, :, :, :].rearrange("p b c s -> p b (c s)"),
                             t_seqs[bass.ds(2 * tile_no(g, c), 2)].rearrange("b p n -> p b n")
                             ).then_inc(tile_loaded[par], 16)
                sp.wait_ge(rows_stored, 32 * (g + c // 2 + 1))
                for w, dst in enumerate((mask1, mask_d)):
                    rows = hot_scratch[w, :, cols].rearrange("e k n -> e (k n)").unsqueeze(1)
                    sp.dma_start(dst[par][:, :], rows.to_broadcast([E, R, TILE])).then_inc(tile_loaded[par], 16)
                for w, dst in enumerate((rho, rstd)):
                    row = scale_scratch[w, cols].rearrange("k n -> (k n)")
                    sp.dma_start(dst[par][:, :], row.partition_broadcast(P)).then_inc(tile_loaded[par], 16)

            def load_x(g, c):
                sp.dma_start(x_out[c % 2][:, :, :],
                             x_rows[bass.ds(KT * tile_no(g, c), KT)].rearrange("k p d -> p k d")
                             ).then_inc(x_loaded[c % 2], 16)

            def store_out(g, c):
                half = KT // 2
                for ready, k in ((out_a_ready, 0), (out_b_ready, half)):
                    sp.wait_ge(ready, tile_no(g, c) + 1)
                    sp.dma_start(out_rows[bass.ds(KT * tile_no(g, c) + k, half)].rearrange("k p d -> p k d"),
                                 x_out[c % 2][:, k:k + half, :]).then_inc(out_stored[c % 2], 16)

            def stored(g, c):
                sp.wait_ge(out_stored[c % 2], 32 * (g + c // 2 + 1))

            sp.wait_ge(wT_ready, JOBS)
            for k in range(2):
                sp.wait_ge(t_stored[k], 16)
            load(0, BATCH - 1)
            store_rows(0)
            load_tile(0, 0, buffers_used=False)
            store(0, TAIL[0] - 1)
            load_tile(0, 1, buffers_used=False)
            for c in TAIL:
                store(0, c)
            for k in range(2):
                sp.wait_ge(t_stored[k], 16 * BATCH // 2)
            sp.wait_ge(gate_ready, BATCH)
            load_x(0, 0)
            load_x(0, 1)

            def tile(g, c, routes=False):
                load_tile(g, c + 1)
                store_out(g, c - 1)
                stored(g, c - 1)
                load_x(g, c + 1)
                if routes:
                    store_rows(group_in(g, c))

            store_rows(1)
            tile(0, 1)
            with sp.Fori(0, TILE_LOOPS) as g:
                tile(g, 2, routes=True)
                tile(g, 3)
            tile(0, TILES - 2)
            store_out(0, TILES - 2)
            store_out(0, TILES - 1)
            stored(0, TILES - 2)
            stored(0, TILES - 1)

        @block.gpsimd
        def _(pool):
            nc.gpsimd.memset(ident[:, :], 0.0).then_inc(const_ready, 1)
            pool.wait_ge(const_ready, 1)
            nc.gpsimd.affine_select(out=ident[:, :], in_=ident[:, :], compare_op=ALU.not_equal, fill=1.0,
                                    base=0, pattern=[[-1, P]], channel_multiplier=1).then_inc(const_ready, 1)
            nc.gpsimd.memset(ones[:, :], 1.0).then_inc(const_ready, 1)
            nc.gpsimd.iota(rank_key[:, :], pattern=[[-1, E]], base=E, channel_multiplier=0,
                           allow_small_or_imprecise_dtypes=True).then_inc(const_ready, 1)
            nc.gpsimd.iota(stage_id[:, :], pattern=[[0, 1]], base=0, channel_multiplier=1,
                           allow_small_or_imprecise_dtypes=True).then_inc(const_ready, 1)

            def value_low(g, c):
                pool.wait_ge(value_hi_ready, seq(g, c) + 1)
                hi, lo = value[c % 2]
                nc.gpsimd.tensor_tensor(lo[:, :, :], kv[c % RING][:, :, :], f32(hi[:, :, :]), ALU.subtract
                                        ).then_inc(value_lo_ready, 1)

            def sum_squares(g, c):
                pool.wait_ge(oT_squared, seq(g, c) + 1)
                nc.gpsimd.tensor_tensor(sq_sum[c % 2][:, :], oT_sq[c % 2][:, 0:S], oT_sq[c % 2][:, S:2 * S], ALU.add
                                        ).then_inc(sq_summed, 1)

            def step(g, c):
                value_low(g, c)
                if c >= 1:
                    sum_squares(g, c - 1)

            for c in HEAD:
                step(0, c)
                if c in B_STEPS:
                    src, dst = ((b1_in, b1_by_j), (b3_in, b3_by_j))[c - B_STEPS[0]]
                    pool.wait_ge(b_loaded, 16 * B_LOADS)
                    nc.gpsimd.tensor_copy(dst[:, :, :, :].rearrange("p j e r -> p e j r"),
                                          src[:, :, :].rearrange("p e (j r) -> p e j r", j=FC)
                                          ).then_inc(b_ordered, 1)
            with pool.Fori(0, LOOPS) as g:
                for c in LOOP:
                    step(g, c)

            def t_low(g, c):
                pool.wait_ge(t_hi_ready, tile_no(g, c) + 1)
                nc.gpsimd.tensor_tensor(t_lo[c % 2][:, :, :], t_scaled[:, :, :], f32(t_hi[c % 2][:, :, :]),
                                        ALU.subtract).then_inc(t_lo_ready, 1)

            for c in TAIL:
                step(0, c)
                if c == T0_STEP:
                    t_low(0, 0)

            def v_low(g, c, k):
                pool.wait_ge(v_hi_ready, 4 * tile_no(g, c) + k + 1)
                nc.gpsimd.tensor_tensor(v_lo[k][:, :], v_full[k][:, :], f32(v_hi[k][:, :]),
                                        ALU.subtract).then_inc(v_lo_ready, 1)

            def add_residual(g, c):
                half = x_out[c % 2][:, KT // 2:KT, :]
                pool.wait_ge(y_scaled_ready, tile_no(g, c) + 1)
                pool.wait_ge(x_loaded[c % 2], 16 * (g + c // 2 + 1))
                nc.gpsimd.tensor_tensor(half, y_scaled[:, :, :], half, ALU.add).then_inc(out_b_ready, 1)

            v_low(0, 0, 0)
            v_low(0, 0, 1)
            sum_squares(0, BATCH - 1)
            v_low(0, 0, 2)
            v_low(0, 0, 3)
            t_low(0, 1)

            def tile(g, c):
                for k in range(4):
                    v_low(g, c, k)
                add_residual(g, c - 1)
                t_low(g, c + 1)

            tile(0, 1)
            with pool.Fori(0, TILE_LOOPS) as g:
                for c in (2, 3):
                    tile(g, c)
            tile(0, TILES - 2)
            for k in range(4):
                v_low(0, TILES - 1, k)
            add_residual(0, TILES - 2)
            add_residual(0, TILES - 1)

        @block.scalar
        def _(act):
            def load_weights():
                for dst, src in ((b1_in[:, :, :], b1.rearrange("e (p j) r -> p e (j r)", j=FC)),
                                 (b3_in[:, :, :], b3.rearrange("e (p j) r -> p e (j r)", j=FC))):
                    act.dma_start(dst, src).then_inc(b_loaded, 16)
                for dst, src in ((a1_in[:, :], a1.rearrange("e r d -> (e r) d")),
                                 (a3_in[:, :], a3.rearrange("e r d -> (e r) d")),
                                 (w1_in[:, :, :], w1.rearrange("(p j) d -> p j d", j=FC)),
                                 (w3_in[:, :, :], w3.rearrange("(p j) d -> p j d", j=FC)),
                                 (w2_in[:, :, :], w2.rearrange("(c p) f -> p c f", p=P)),
                                 (a2_in[:, :], a2.rearrange("e r f -> (e r) f")),
                                 (b2_in[:, 0], b2[:, 0:P, :].rearrange("e p r -> p e r")),
                                 (b2_in[:, 1], b2[:, P:D, :].rearrange("e p r -> p e r"))):
                    act.dma_start(dst, src).then_inc(w_loaded, 16)

            def weight_high(i, k):
                n = job_no(i, k)
                act.wait_ge(wT_ready, n + 1)
                for col, cols, hi, lo, scale in jobs[n][1]:
                    last = nc.scalar.activation(hi, w_bank[n % 2][:, col:col + cols], ACT.Copy, scale=scale)
                last.then_inc(w_hi_ready, 1)

            def qk_high(g, c):
                act.wait_ge(qkT_ready, seq(g, c) + 1)
                nc.scalar.activation(qT[c % 2][0][:, :], qT_bank[:, :], ACT.Copy).then_inc(qT_hi_ready, 1)
                nc.scalar.activation(kT[c % 2][0][:, :], kT_bank[:, :], ACT.Copy).then_inc(kT_hi_ready, 1)

            def value_high(g, c):
                act.wait_ge(seq_loaded[c % RING], 32 * (g + c // RING + 1))
                nc.scalar.activation(value[c % 2][0][:, :, :], kv[c % RING][:, :, :], ACT.Copy
                                     ).then_inc(value_hi_ready, 1)

            def exp(g, c):
                act.wait_ge(max_ready, seq(g, c) + 1)
                for h in range(SC):
                    last = nc.scalar.activation(prob[c % 2][:, h, :], score_bank[:, h * S:(h + 1) * S], ACT.Exp,
                                                bias=neg_max[c % 2][:, h:h + 1],
                                                accum_out=row_sum[c % RING][:, h:h + 1])
                last.then_inc(prob_ready, 1)

            def probT_high(g, c):
                act.wait_ge(probT_ready, seq(g, c) + 1)
                nc.scalar.activation(probT[c % 2][0][:, :], probT_bank[:, :], ACT.Copy).then_inc(probT_hi_ready, 1)

            def copy_oT(g, c):
                act.wait_ge(o_ready, seq(g, c) + 1)
                if c >= 2:
                    act.wait_ge(t_stored[c % 2], 16 * (2 * g + c // 2))
                nc.scalar.activation(oT[c % 2][:, :], o_bank[:, :], ACT.Copy).then_inc(oT_copied, 1)
                nc.scalar.activation(oT_sq[c % 2][:, :], o_bank[:, :], ACT.Square).then_inc(oT_squared, 1)

            def exp_gap(r):
                act.wait_ge(gap_ready, r + 1)
                nc.scalar.activation(scales[:, 0, :], g_t[:, :], ACT.Exp).then_inc(rho_ready, 1)

            def copy_rows(r, src, first=False):
                act.wait_ge(rows_ready, r + 1)
                if not first:
                    act.wait_ge(rows_stored, 32 * r)
                nc.scalar.activation(hot_rows[:, :], src[:, 0:P], ACT.Copy)
                nc.scalar.activation(scale_rows[:, :], src[0:2 * GCOLS, P:2 * P], ACT.Copy).then_inc(rows_copied, 1)

            def step(g, c, jobs_here=False):
                if jobs_here:
                    weight_high(c, 0)
                if not isinstance(g, int) or c + 1 < BATCH:
                    qk_high(g, c + 1)
                if jobs_here:
                    weight_high(c, 1)
                exp(g, c)
                value_high(g, c)
                if c >= 1:
                    copy_oT(g, c - 1)
                if jobs_here:
                    weight_high(c, 2)
                probT_high(g, c)
                if jobs_here:
                    weight_high(c, 3)

            qk_high(0, 0)
            load_weights()
            act.wait_ge(gate_wT_ready, 1)
            for c in range(DC):
                last = nc.scalar.activation(gateT[:, c, :], row_bank[:, c * E:(c + 1) * E], ACT.Copy,
                                            scale=nw_at(c))
            last.then_inc(gate_w_copied, 1)
            for c in HEAD:
                step(0, c, c in JOB_STEPS)
                if c == ROUTE_STEP + 2:
                    exp_gap(0)
            with act.Fori(0, LOOPS) as g:
                for c in LOOP:
                    step(g, c)

            def t_high(g, c):
                act.wait_ge(t_scaled_ready, tile_no(g, c) + 1)
                nc.scalar.activation(t_hi[c % 2][:, :, :], t_scaled[:, :, :], ACT.Copy).then_inc(t_hi_ready, 1)

            def v_high(g, c, k):
                act.wait_ge(v_ready, 4 * tile_no(g, c) + k + 1)
                nc.scalar.activation(v_hi[k][:, :], v_full[k][:, :], ACT.Copy).then_inc(v_hi_ready, 1)

            def first_silu(g, c, j):
                act.wait_ge(h1_first, chunk_no(g, c, j) + 1)
                nc.scalar.activation(silu_a[j % 2][:, :], h1_bank[j % 2][:, :], ACT.Silu).then_inc(silu_a_ready, 1)

            def second_silu(g, c, j):
                act.wait_ge(h1_second, chunk_no(g, c, j) + 1)
                nc.scalar.activation(silu_b[:, :], h1_bank[j % 2][:, :], ACT.Silu).then_inc(silu_b_ready, 1)

            def down_high(g, c, j, buffer_used=True):
                n = chunk_no(g, c, j)
                if buffer_used:
                    act.wait_ge(down_done, n - 1)
                act.wait_ge(act_s_ready, n + 1)
                nc.scalar.activation(s_hi[j % 2][:, :], act_s[j % 2][:, :], ACT.Copy).then_inc(s_hi_ready, 1)
                act.wait_ge(act_br_ready, n + 1)
                nc.scalar.activation(br_hi[j % 2][:, :], act_br[j % 2][:, :], ACT.Copy).then_inc(br_hi_ready, 1)

            def z_high(g, c):
                act.wait_ge(z_ready, tile_no(g, c) + 1)
                nc.scalar.activation(z_hi[:, :], z_a[:, :], ACT.Copy).then_inc(z_hi_ready, 1)

            def copy_y0(g, c):
                act.wait_ge(y_ready, tile_no(g, c) + 1)
                nc.scalar.activation(yT[:, 0, :], y_bank[0][:, :], ACT.Copy).then_inc(y0_copied, 1)

            def scale_y(g, c):
                act.wait_ge(yT_ready, 2 * tile_no(g, c) + 1)
                act.wait_ge(rt_ready, tile_no(g, c) + 1)
                for k in range(KT // 2, KT):
                    last = nc.scalar.activation(y_scaled[:, k - KT // 2, :], h3_bank[0][:, (k % 2) * D:(k % 2 + 1) * D],
                                                ACT.Copy, scale=rt[c % 2][:, k:k + 1])
                last.then_inc(y_scaled_ready, 1)

            def act_tile(g, c, first=False, last=False, routes=False):
                v_high(g, c, 0)
                v_high(g, c, 1)
                if first:
                    copy_oT(0, BATCH - 1)
                else:
                    second_silu(g, c - 1, FC - 1)
                    act.wait_ge(h3_second, chunk_no(g, c))
                v_high(g, c, 2)
                v_high(g, c, 3)
                if not first:
                    down_high(g, c - 1, FC - 1)
                first_silu(g, c, 0)
                if not first:
                    z_high(g, c - 1)
                for j in range(1, FC):
                    first_silu(g, c, j)
                    if j == 2 and not first:
                        copy_y0(g, c - 1)
                    second_silu(g, c, j - 1)
                    if j == 3 and not first:
                        scale_y(g, c - 1)
                    if j == 7 and routes:
                        copy_rows(group_in(g, c), h1_bank[0])
                    down_high(g, c, j - 1, buffer_used=not (first and j < 3))
                    if j == 4 and routes:
                        exp_gap(group_in(g, c))
                    if j == 6 and not last:
                        t_high(g, c + 1)

            copy_rows(0, row_bank, first=True)
            for c in TAIL:
                step(0, c)
                if c == T0_STEP:
                    t_high(0, 0)
            act_tile(0, 0, first=True, routes=True)
            act_tile(0, 1)
            with act.Fori(0, TILE_LOOPS) as g:
                act_tile(g, 2, routes=True)
                act_tile(g, 3)
            end = TILES - 1
            act_tile(0, end - 1)
            act_tile(0, end, last=True)
            second_silu(0, end, FC - 1)
            down_high(0, end, FC - 1)
            z_high(0, end)
            copy_y0(0, end)
            act.wait_ge(out_b_ready, end)
            scale_y(0, end)

        @block.vector
        def _(dve):
            dve.wait_ge(stage_loaded, 16 * STAGE_LOADS)
            dve.wait_ge(const_ready, 5)
            nc.vector.tensor_copy(itok_f[:, :], itok_in[:, :]).then_inc(stage_ready, 1)
            dve.wait_ge(stage_ready, 1)
            nc.vector.tensor_scalar(stage_hot[:, :], itok_f[:, :], stage_id[:, 0:1], None, ALU.is_equal
                                    ).then_inc(stage_ready, 1)
            dve.wait_ge(bias_ready, 1)
            nc.vector.tensor_copy(bias[:, :, :].rearrange("p h b -> p (h b)"), bias_bank[:, 0:SC * BATCH]
                                  ).then_inc(bias_copied, 1)
            dve.wait_ge(bias_copied, 1)

            def weight_low(i, k):
                n = job_no(i, k)
                dve.wait_ge(w_hi_ready, n + 1)
                for col, cols, hi, lo, scale in jobs[n][1]:
                    last = nc.vector.scalar_tensor_tensor(lo, w_bank[n % 2][:, col:col + cols], scale, f32(hi),
                                                          ALU.mult, ALU.subtract)
                last.then_inc(w_lo_ready, 1)

            def add_bias(g, c, buffer_used=True):
                if buffer_used:
                    dve.wait_ge(qkT_ready, seq(g, c) - 1)
                dve.wait_ge(seq_loaded[c % RING], 32 * (g + c // RING + 1))
                for h in range(SC):
                    last = nc.vector.tensor_scalar(q[c % 2][:, h, :], x_in[c % RING][:, h, :],
                                                   bias[:, h, bass.ds(seq(g, c), 1)], None, ALU.add)
                last.then_inc(q_ready, 1)

            def qk_low(g, c):
                dve.wait_ge(qT_hi_ready, seq(g, c) + 1)
                nc.vector.tensor_tensor(qT[c % 2][1][:, :], qT_bank[:, :], f32(qT[c % 2][0][:, :]), ALU.subtract)
                dve.wait_ge(kT_hi_ready, seq(g, c) + 1)
                nc.vector.tensor_tensor(kT[c % 2][1][:, :], kT_bank[:, :], f32(kT[c % 2][0][:, :]), ALU.subtract
                                        ).then_inc(qkT_lo_ready, 1)

            def row_max(g, c):
                dve.wait_ge(scores_ready, seq(g, c) + 1)
                nc.vector.tensor_reduce(neg_max[c % 2][:, :], score_bank[:, :].rearrange("p (h t) -> p h t", h=SC),
                                        AXIS.X, ALU.max, negate=True).then_inc(max_ready, 1)

            def probT_low(g, c):
                dve.wait_ge(probT_hi_ready, seq(g, c) + 1)
                nc.vector.tensor_tensor(probT[c % 2][1][:, :], probT_bank[:, :], f32(probT[c % 2][0][:, :]),
                                        ALU.subtract).then_inc(probT_lo_ready, 1)

            def keep_gate(g, c):
                dve.wait_ge(gate_ready, seq(g, c) + 1)
                r = row_sum[c % RING]
                cols = bass.ds(SC * seq(g, c), SC)
                nc.vector.scalar_tensor_tensor(eps_r2[:, :], r[:, :], EPS, r[:, :], ALU.mult, ALU.mult
                                               ).then_inc(eps_ready, 1)
                dve.wait_ge(eps_ready, seq(g, c) + 1)
                halves = gate_bank[:, 0:SC * GATE_STRIDE].rearrange("p (h n) -> p h n", h=SC)
                nc.vector.scalar_tensor_tensor(mean_sq[:, cols], halves[:, :, E], 1.0 / D,
                                               eps_r2[:, :], ALU.mult, ALU.add)
                nc.vector.tensor_scalar(logits[:, cols, :], halves[:, :, 0:E], 1.0, None,
                                        ALU.mult).then_inc(gate_read, 1)

            ROUTE_OPS = 30

            def link(r, k, ins):
                ins.then_inc(route_chain, 1)
                dve.wait_ge(route_chain, ROUTE_OPS * r + k)

            def bcast(ap):
                return ap.unsqueeze(2).to_broadcast([P, GCOLS, E])

            rank = rank_key[:, :].unsqueeze(1).to_broadcast([P, GCOLS, E])

            def pick(r, k, best, hot):
                link(r, k, nc.vector.tensor_reduce(best[:, :], g_logits[:, :, :], AXIS.X, ALU.max))
                link(r, k + 1, nc.vector.tensor_tensor(g_key[:, :, :], g_logits[:, :, :], bcast(best[:, :]), ALU.is_equal))
                link(r, k + 2, nc.vector.tensor_tensor(g_key[:, :, :], g_key[:, :, :], rank, ALU.mult))
                link(r, k + 3, nc.vector.tensor_reduce(g_best[:, :], g_key[:, :, :], AXIS.X, ALU.max))
                link(r, k + 4, nc.vector.tensor_tensor(hot[:, :, :], g_key[:, :, :], bcast(g_best[:, :]), ALU.is_equal))

            def route_first(r):
                cols = bass.ds(GCOLS * r, GCOLS)
                dve.wait_ge(gate_read, GROUP * r + GROUP)
                link(r, 1, nc.vector.tensor_scalar(g_logits[:, :, :], logits[:, cols, :], 1.0, None, ALU.mult))
                link(r, 2, nc.vector.tensor_scalar(g_z[:, :], mean_sq[:, cols], 1.0, None, ALU.mult))
                pick(r, 3, g_top1, g_hot1)

            def route_second(r, first=False):
                link(r, 8, nc.vector.scalar_tensor_tensor(g_logits[:, :, :], g_hot1[:, :, :], -3.0e38,
                                                          g_logits[:, :, :], ALU.mult, ALU.add))
                pick(r, 9, g_top2, g_hot2)
                if not first:
                    dve.wait_ge(rows_ready, r)
                link(r, 14, nc.vector.tensor_copy(hots[:, 0].rearrange("p e c -> p c e"), g_hot1[:, :, :]))
                link(r, 15, nc.vector.tensor_tensor(hots[:, 1].rearrange("p e c -> p c e"), g_hot2[:, :, :], g_hot1[:, :, :], ALU.subtract))

            def route_rstd(r):
                y_bits, z_bits = g_y[:, :].bitcast(I32), g_z[:, :].bitcast(I32)
                link(r, 16, nc.vector.tensor_scalar(y_bits, z_bits, 1, None, ALU.logical_shift_right))
                link(r, 17, nc.vector.tensor_scalar(y_bits, y_bits, -1.0, RSQRT_SEED, ALU.mult, ALU.add))
                for n in range(3):
                    target = scales[:, 1] if n == 2 else g_y[:, :]
                    link(r, 18 + 3 * n, nc.vector.tensor_tensor(g_t[:, :], g_y[:, :], g_y[:, :], ALU.mult))
                    link(r, 19 + 3 * n, nc.vector.scalar_tensor_tensor(g_t[:, :], g_t[:, :], -0.5, g_z[:, :],
                                                                       ALU.mult, ALU.mult))
                    link(r, 20 + 3 * n, nc.vector.scalar_tensor_tensor(target, g_t[:, :], 1.5, g_y[:, :],
                                                                       ALU.add, ALU.mult))

            def route_gap(r):
                link(r, 27, nc.vector.tensor_tensor(g_t[:, :], g_top2[:, :], g_top1[:, :], ALU.subtract))
                nc.vector.tensor_tensor(g_t[:, :], g_t[:, :], scales[:, 1], ALU.mult).then_inc(gap_ready, 1)

            def route_weight(r):
                dve.wait_ge(rho_ready, r + 1)
                link(r, 28, nc.vector.tensor_scalar(g_y[:, :], scales[:, 0], 1.0, None, ALU.add))
                link(r, 29, nc.vector.reciprocal(g_y[:, :], g_y[:, :]))
                link(r, 30, nc.vector.tensor_scalar(w_first[:, bass.ds(GCOLS * r, GCOLS)], g_y[:, :], 1.0, None, ALU.mult))

            def scale_t(g, c, buffer_used=True):
                dve.wait_ge(tile_loaded[c % 2], TILE_LOADS * (g + c // 2 + 1))
                if buffer_used:
                    dve.wait_ge(t_lo_ready, tile_no(g, c))
                for dc in range(DC):
                    last = nc.vector.tensor_tensor(t_scaled[:, dc, :].rearrange("p (b s) -> p b s", b=2),
                                                   t_in[c % 2][:, :, dc, :],
                                                   rstd[c % 2][:, :].rearrange("p (b s) -> p b s", b=2), ALU.mult)
                last.then_inc(t_scaled_ready, 1)

            def load_weight(g, c, buffer_used=True):
                if buffer_used:
                    dve.wait_ge(out_a_ready, tile_no(g, c) - 1)
                    dve.wait_ge(y_scaled_ready, tile_no(g, c) - 1)
                nc.vector.tensor_scalar(rt[c % 2][:, :], w_first[:, bass.ds(KT * tile_no(g, c), KT)], 1.0, None,
                                        ALU.mult).then_inc(rt_ready, 1)

            def beside(c):
                if c == ROUTE_STEP:
                    route_first(0)
                if c == ROUTE_STEP + 1:
                    route_second(0, first=True)
                if c == ROUTE_STEP + 2:
                    route_rstd(0)
                    route_gap(0)
                if c == TAIL[0]:
                    route_weight(0)
                if c == T0_STEP:
                    scale_t(0, 0, buffer_used=False)
                    load_weight(0, 0, buffer_used=False)

            def step(g, c, jobs_here=False, peeled=False):
                row_max(g, c)
                if jobs_here:
                    weight_low(c, 0)
                if peeled:
                    beside(c)
                if not isinstance(g, int) or c + 1 < BATCH:
                    qk_low(g, c + 1)
                if jobs_here:
                    weight_low(c, 1)
                if c >= 2:
                    keep_gate(g, c - 2)
                if not isinstance(g, int) or c + 2 < BATCH:
                    add_bias(g, c + 2)
                if jobs_here:
                    weight_low(c, 2)
                probT_low(g, c)
                if jobs_here:
                    weight_low(c, 3)

            add_bias(0, 0, buffer_used=False)
            add_bias(0, 1, buffer_used=False)
            qk_low(0, 0)
            for c in HEAD:
                step(0, c, c in JOB_STEPS, peeled=True)
            with dve.Fori(0, LOOPS) as g:
                for c in LOOP:
                    step(g, c)

            def mask_u(g, c, first=False):
                dve.wait_ge(u_ready, tile_no(g, c) + 1)
                if first:
                    dve.wait_ge(value_lo_ready, BATCH)
                else:
                    dve.wait_ge(v_lo_ready, 4 * tile_no(g, c))
                for k in range(4):
                    u = (h1_bank[0], h3_bank[0])[k % 2]
                    m = (mask1, mask_d)[k // 2][c % 2]
                    nc.vector.tensor_tensor(v_full[k][:, :], u[:, :], m[:, :], ALU.mult).then_inc(v_ready, 1)

            def first_act(g, c, j):
                dve.wait_ge(h3_first, chunk_no(g, c, j) + 1)
                dve.wait_ge(silu_a_ready, chunk_no(g, c, j) + 1)
                nc.vector.tensor_tensor(act_a[j % 2][:, :], silu_a[j % 2][:, :], h3_bank[j % 2][:, :], ALU.mult
                                        ).then_inc(act_a_ready, 1)

            def second_act(g, c, j):
                n = chunk_no(g, c, j)
                dve.wait_ge(h3_second, n + 1)
                dve.wait_ge(silu_b_ready, n + 1)
                nc.vector.tensor_tensor(act_b[:, :], silu_b[:, :], h3_bank[j % 2][:, :], ALU.mult
                                        ).then_inc(act_b_ready, 1)
                dve.wait_ge(act_b_ready, n + 1)
                nc.vector.tensor_tensor(act_br[j % 2][:, :], act_b[:, :], rho[c % 2][:, :], ALU.mult
                                        ).then_inc(act_br_ready, 1)
                dve.wait_ge(act_br_ready, n + 1)
                dve.wait_ge(act_a_ready, n + 1)
                nc.vector.tensor_tensor(act_s[j % 2][:, :], act_a[j % 2][:, :], act_br[j % 2][:, :], ALU.add
                                        ).then_inc(act_s_ready, 1)

            def down_low(g, c, j):
                n = chunk_no(g, c, j)
                dve.wait_ge(s_hi_ready, n + 1)
                nc.vector.tensor_tensor(s_lo[j % 2][:, :], act_s[j % 2][:, :], f32(s_hi[j % 2][:, :]), ALU.subtract)
                dve.wait_ge(br_hi_ready, n + 1)
                nc.vector.tensor_tensor(br_lo[j % 2][:, :], act_br[j % 2][:, :], f32(br_hi[j % 2][:, :]), ALU.subtract
                                        ).then_inc(down_in_ready, 1)

            def mask_z(g, c):
                n = tile_no(g, c) + 1
                dve.wait_ge(z_in_ready, n)
                nc.vector.tensor_tensor(z_b[:, :], ba_bank[:, :], mask_d[c % 2][:, :], ALU.mult).then_inc(z_b_ready, 1)
                nc.vector.tensor_tensor(z_a[:, :], sa_bank[:, :], mask1[c % 2][:, :], ALU.mult).then_inc(z_a_ready, 1)
                dve.wait_ge(z_b_ready, n)
                dve.wait_ge(z_a_ready, n)
                nc.vector.tensor_tensor(z_a[:, :], z_a[:, :], z_b[:, :], ALU.add).then_inc(z_ready, 1)
                dve.wait_ge(z_hi_ready, n)
                nc.vector.tensor_tensor(z_lo[:, :], z_a[:, :], f32(z_hi[:, :]), ALU.subtract).then_inc(z_lo_ready, 1)

            def copy_y1(g, c):
                dve.wait_ge(y_ready, tile_no(g, c) + 1)
                nc.vector.tensor_copy(yT[:, 1, :], y_bank[1][:, :]).then_inc(y1_copied, 1)

            def add_residual(g, c):
                dve.wait_ge(yT_ready, 2 * tile_no(g, c) + 2)
                dve.wait_ge(x_loaded[c % 2], 16 * (g + c // 2 + 1))
                for k in range(KT // 2):
                    last = nc.vector.scalar_tensor_tensor(x_out[c % 2][:, k, :], h1_bank[0][:, k * D:(k + 1) * D],
                                                          rt[c % 2][:, k:k + 1], x_out[c % 2][:, k, :],
                                                          ALU.mult, ALU.add)
                last.then_inc(out_a_ready, 1)

            def dve_tile(g, c, first=False, last=False, routes=False):
                mask_u(g, c, first)
                if first:
                    keep_gate(0, BATCH - 2)
                    keep_gate(0, BATCH - 1)
                else:
                    second_act(g, c - 1, FC - 1)
                    down_low(g, c - 1, FC - 1)
                first_act(g, c, 0)
                if not first:
                    mask_z(g, c - 1)
                for j in range(1, FC):
                    first_act(g, c, j)
                    if j == 2 and not first:
                        copy_y1(g, c - 1)
                    second_act(g, c, j - 1)
                    if j == 3 and not first:
                        add_residual(g, c - 1)
                    if j == 5 and not last:
                        scale_t(g, c + 1)
                        load_weight(g, c + 1, buffer_used=not first)
                    down_low(g, c, j - 1)
                    if j == 2 and routes:
                        route_first(group_in(g, c))
                    if j == 3 and routes:
                        route_second(group_in(g, c))
                    if j == 4 and routes:
                        route_rstd(group_in(g, c))
                        route_gap(group_in(g, c))
                    if j == 6 and routes:
                        route_weight(group_in(g, c))
                    if j == 4 and first:
                        for k in range(2):
                            dve.wait_ge(t_stored[k], 16 * BATCH // 2)

            for c in TAIL:
                step(0, c, peeled=True)
            dve_tile(0, 0, first=True, routes=True)
            dve_tile(0, 1)
            with dve.Fori(0, TILE_LOOPS) as g:
                dve_tile(g, 2, routes=True)
                dve_tile(g, 3)
            end = TILES - 1
            dve_tile(0, end - 1)
            dve_tile(0, end, last=True)
            second_act(0, end, FC - 1)
            down_low(0, end, FC - 1)
            mask_z(0, end)
            copy_y1(0, end)
            add_residual(0, end)

        @block.tensor
        def _(pe):
            def product(dst, w, x_parts, start, stop, grouped=True):
                (w_hi, w_lo), (x_hi, x_lo) = w, x_parts
                nc.tensor.matmul(dst, w_hi, x_hi, start=start, stop=False, skip_group_check=not grouped)
                nc.tensor.matmul(dst, w_hi, x_lo, start=False, stop=False, skip_group_check=not grouped)
                return nc.tensor.matmul(dst, w_lo, x_hi, start=False, stop=stop, skip_group_check=not grouped)

            def at(parts, *index):
                return parts[0][index], parts[1][index]

            ALL = slice(None)

            pe.wait_ge(const_ready, 5)
            pe.wait_ge(stage_loaded, 16 * STAGE_LOADS)
            pe.wait_ge(stage_ready, 2)
            for h in range(SC):
                last = nc.tensor.matmul(bias_bank[:, h * BATCH:(h + 1) * BATCH], embed_in[:, h * P:(h + 1) * P],
                                        stage_hot[:, :], start=True, stop=True)
            last.then_inc(bias_ready, 1)

            def weight_job(i, k):
                n = job_no(i, k)
                if n == 0:
                    pe.wait_ge(w_loaded, 16 * W_LOADS)
                    pe.wait_ge(gate_w_copied, 1)
                    pe.wait_ge(bias_copied, 1)
                if n == FIRST_B_JOB:
                    pe.wait_ge(b_ordered, 2)
                if n >= 2:
                    pe.wait_ge(w_lo_ready, n - 1)
                for col, cols, src, rows in jobs[n][0]:
                    last = nc.tensor.transpose(w_bank[n % 2][0:P, col:col + cols], src, ident[0:rows, 0:rows])
                last.then_inc(wT_ready, 1)

            def transpose_qk(g, c):
                pe.wait_ge(q_ready, seq(g, c) + 1)
                for src, dst in ((q[c % 2], qT_bank), (kv[c % RING], kT_bank)):
                    for dc in range(DC):
                        for h in range(SC):
                            last = nc.tensor.transpose(dst[:, dc * S + h * P:dc * S + (h + 1) * P],
                                                       src[:, h, dc * P:(dc + 1) * P], ident[:, :])
                last.then_inc(qkT_ready, 1)

            def scores(g, c):
                pe.wait_ge(qkT_lo_ready, seq(g, c) + 1)
                for h in range(SC):
                    for dc in range(DC):
                        last = product(score_bank[:, h * S:(h + 1) * S],
                                       at(qT[c % 2], ALL, slice(dc * S + h * P, dc * S + (h + 1) * P)),
                                       at(kT[c % 2], ALL, slice(dc * S, (dc + 1) * S)), dc == 0, dc == DC - 1)
                last.then_inc(scores_ready, 1)

            def transpose_prob(g, c):
                pe.wait_ge(prob_ready, seq(g, c) + 1)
                for tc in range(SC):
                    for h in range(SC):
                        last = nc.tensor.transpose(probT_bank[:, tc * S + h * P:tc * S + (h + 1) * P],
                                                   prob[c % 2][:, h, tc * P:(tc + 1) * P], ident[:, :])
                last.then_inc(probT_ready, 1)

            def attend(g, c):
                pe.wait_ge(value_lo_ready, seq(g, c) + 1)
                pe.wait_ge(probT_lo_ready, seq(g, c) + 1)
                for dc in range(DC):
                    for tc in range(SC):
                        last = product(o_bank[:, dc * S:(dc + 1) * S],
                                       at(value[c % 2], ALL, tc, slice(dc * P, (dc + 1) * P)),
                                       at(probT[c % 2], ALL, slice(tc * S, (tc + 1) * S)), tc == 0, tc == SC - 1)
                last.then_inc(o_ready, 1)

            def gate(g, c, first=False):
                if first:
                    pe.wait_ge(gate_w_copied, 1)
                else:
                    pe.wait_ge(gate_read, seq(g, c))
                pe.wait_ge(oT_copied, seq(g, c) + 1)
                for h in range(SC):
                    for dc in range(DC):
                        nc.tensor.matmul(gate_bank[:, h * GATE_STRIDE:h * GATE_STRIDE + E],
                                         oT[c % 2][:, dc * S + h * P:dc * S + (h + 1) * P],
                                         gateT[:, dc, :], start=(dc == 0), stop=(dc == DC - 1))
                pe.wait_ge(sq_summed, seq(g, c) + 1)
                for h in range(SC):
                    col = h * GATE_STRIDE + E
                    last = nc.tensor.matmul(gate_bank[:, col:col + 1], sq_sum[c % 2][:, h * P:(h + 1) * P],
                                            ones[:, :], start=True, stop=True)
                last.then_inc(gate_ready, 1)

            def transpose_rows(r, dst):
                pe.wait_ge(rho_ready, r + 1)
                nc.tensor.transpose(dst[:, 0:P], hots[:, :, :, :].rearrange("p w e c -> p (w e c)"), ident[:, :])
                nc.tensor.transpose(dst[0:2 * GCOLS, P:2 * P], scales[:, :, :].rearrange("p w c -> p (w c)"),
                                    ident[:, :]).then_inc(rows_ready, 1)

            def step(g, c, jobs_here=False):
                scores(g, c)
                if jobs_here:
                    weight_job(c, 0)
                if not isinstance(g, int) or c + 1 < BATCH:
                    transpose_qk(g, c + 1)
                if jobs_here:
                    weight_job(c, 1)
                if c >= 2:
                    gate(g, c - 2, first=isinstance(g, int) and c == 2)
                if c >= 1:
                    attend(g, c - 1)
                if jobs_here:
                    weight_job(c, 2)
                transpose_prob(g, c)
                if jobs_here:
                    weight_job(c, 3)

            transpose_qk(0, 0)
            pe.wait_ge(gate_loaded, 16 * GATE_LOADS)
            for c in range(DC):
                last = nc.tensor.transpose(row_bank[:, c * E:(c + 1) * E], gate_in[:, c * P:(c + 1) * P],
                                           ident[0:E, 0:E])
            last.then_inc(gate_wT_ready, 1)
            for c in HEAD:
                step(0, c, c in JOB_STEPS)
            with pe.Fori(0, LOOPS) as g:
                for c in LOOP:
                    step(g, c)
            pe.wait_ge(w_lo_ready, JOBS)
            transpose_rows(0, row_bank)
            for c in TAIL:
                step(0, c)

            def low_rank(g, c):
                pe.wait_ge(t_lo_ready, tile_no(g, c) + 1)
                for w, dst in ((0, h1_bank[0]), (1, h3_bank[0])):
                    for dc in range(DC):
                        last = product(dst[:, :], at(a13T, ALL, dc, w), (t_hi[c % 2][:, dc], t_lo[c % 2][:, dc]),
                                       dc == 0, dc == DC - 1)
                last.then_inc(u_ready, 1)

            def first_expert(g, c, j):
                f = slice(j * P, (j + 1) * P)
                for wT, bT, dst, k, done in ((w1T, b1T, h1_bank[j % 2], 0, h1_first),
                                             (w3T, b3T, h3_bank[j % 2], 1, h3_first)):
                    for dc in range(DC):
                        product(dst[:, :], at(wT, ALL, dc, f), (t_hi[c % 2][:, dc], t_lo[c % 2][:, dc]), dc == 0, False)
                    if j == 0:
                        pe.wait_ge(v_lo_ready, 4 * tile_no(g, c) + k + 1)
                    product(dst[:, :], at(bT, ALL, f), (v_hi[k][:, :], v_lo[k][:, :]), False, True).then_inc(done, 1)

            def second_expert(g, c, j):
                if j == 0:
                    pe.wait_ge(v_lo_ready, 4 * tile_no(g, c) + 4)
                pe.wait_ge(act_a_ready, chunk_no(g, c, j) + 1)
                f = slice(j * P, (j + 1) * P)
                for bT, dst, k, done in ((b1T, h1_bank[j % 2], 2, h1_second), (b3T, h3_bank[j % 2], 3, h3_second)):
                    product(dst[:, :], at(bT, ALL, f), (v_hi[k][:, :], v_lo[k][:, :]), False, True, grouped=False
                            ).then_inc(done, 1)

            def down_y(g, c, j):
                pe.wait_ge(down_in_ready, chunk_no(g, c, j) + 1)
                for half in range(DC):
                    last = product(y_bank[half][:, :], at(w2T, ALL, j, slice(half * P, (half + 1) * P)),
                                   (s_hi[j % 2][:, :], s_lo[j % 2][:, :]), j == 0, False)
                return last

            def down_z(g, c, j):
                pe.wait_ge(down_in_ready, chunk_no(g, c, j) + 1)
                product(sa_bank[:, :], at(a2T, ALL, j), (s_hi[j % 2][:, :], s_lo[j % 2][:, :]), j == 0, j == FC - 1)
                return product(ba_bank[:, :], at(a2T, ALL, j), (br_hi[j % 2][:, :], br_lo[j % 2][:, :]),
                               j == 0, j == FC - 1)

            def finish_y(g, c):
                pe.wait_ge(z_lo_ready, tile_no(g, c) + 1)
                for half in range(DC):
                    last = product(y_bank[half][:, :], at(b2T, ALL, slice(half * P, (half + 1) * P)),
                                   (z_hi[:, :], z_lo[:, :]), False, True)
                last.then_inc(y_ready, 1)

            def transpose_y(g, c):
                for dst, ks in ((h3_bank[0], (2, 3)), (h1_bank[0], (0, 1))):
                    for k in ks:
                        for half in range(DC):
                            col = (k % 2) * D + half * P
                            last = nc.tensor.transpose(dst[:, col:col + P], yT[:, half, k * P:(k + 1) * P], ident[:, :])
                    last.then_inc(yT_ready, 1)

            def wait_y_copied(g, c):
                pe.wait_ge(y0_copied, tile_no(g, c) + 1)
                pe.wait_ge(y1_copied, tile_no(g, c) + 1)

            def pe_tile(g, c, first=False, routes=False, routed=False):
                n = chunk_no(g, c)
                if not first:
                    pe.wait_ge(act_b_ready, n - 1)
                if routed:
                    pe.wait_ge(rows_copied, group_in(g, c) + 1)
                low_rank(g, c)
                if first:
                    gate(0, BATCH - 2)
                    attend(0, BATCH - 1)
                else:
                    second_expert(g, c - 1, FC - 1)
                    down_y(g, c - 1, FC - 2)
                    down_z(g, c - 1, FC - 2).then_inc(down_done, 1)
                pe.wait_ge(v_ready, 4 * tile_no(g, c) + 4)
                first_expert(g, c, 0)
                if first:
                    gate(0, BATCH - 1)
                else:
                    down_z(g, c - 1, FC - 1).then_inc(z_in_ready, 1)
                for j in range(1, FC):
                    if j == 4 and not first:
                        pe.wait_ge(out_a_ready, tile_no(g, c))
                        pe.wait_ge(y_scaled_ready, tile_no(g, c))
                    elif not (first and j == 1):
                        pe.wait_ge(act_b_ready, n + j - 1)
                    first_expert(g, c, j)
                    if j == 2 and not first:
                        finish_y(g, c - 1)
                    second_expert(g, c, j - 1)
                    if j == 1 and not first:
                        down_y(g, c - 1, FC - 1).then_inc(down_done, 1)
                    if j == 2:
                        if first:
                            pe.wait_ge(gate_read, BATCH)
                            pe.wait_ge(rows_copied, 1)
                        down_z(g, c, 0)
                        if not first:
                            wait_y_copied(g, c - 1)
                        down_y(g, c, 0).then_inc(down_done, 1)
                    elif j == 3:
                        down_y(g, c, 1)
                        if not first:
                            pe.wait_ge(act_b_ready, n + 3)
                            transpose_y(g, c - 1)
                        down_z(g, c, 1).then_inc(down_done, 1)
                    elif j >= 4:
                        down_y(g, c, j - 2)
                        if j == 7 and routes:
                            pe.wait_ge(act_b_ready, n + 7)
                            transpose_rows(group_in(g, c), h1_bank[0])
                        down_z(g, c, j - 2).then_inc(down_done, 1)

            pe_tile(0, 0, first=True, routes=True)
            pe_tile(0, 1, routed=True)
            with pe.Fori(0, TILE_LOOPS) as g:
                pe_tile(g, 2, routes=True)
                pe_tile(g, 3, routed=True)
            end = TILES - 1
            pe_tile(0, end - 1)
            pe_tile(0, end)
            second_expert(0, end, FC - 1)
            down_y(0, end, FC - 2)
            down_z(0, end, FC - 2).then_inc(down_done, 1)
            down_z(0, end, FC - 1).then_inc(z_in_ready, 1)
            down_y(0, end, FC - 1).then_inc(down_done, 1)
            finish_y(0, end)
            pe.wait_ge(act_b_ready, chunk_no(0, end, FC))
            wait_y_copied(0, end)
            transpose_y(0, end)


_INS = ['x', 'fside_BxSxS_0', 'itok_B_0_5', 'L0_cond_braak_embed', 'L0_ffn_norm_w', 'L0_ffn_w1', 'L0_ffn_w3',
        'L0_ffn_w2', 'L0_ffn_gate_w', 'L0_ffn_a1', 'L0_ffn_b1', 'L0_ffn_a3', 'L0_ffn_b3', 'L0_ffn_a2', 'L0_ffn_b2']


def kernel(**inputs):
    import numpy as np
    import concourse.bacc as bacc
    from concourse.bass_utils import run_bass_kernel_spmd

    nc = bacc.Bacc("TRN2", target_bir_lowering=False, num_devices=1)
    arrays, args = {}, []
    for name in _INS:
        a = np.ascontiguousarray(inputs[name])
        arrays[f"in_{name}"] = a
        args.append(nc.dram_tensor(f"in_{name}", a.shape, mybir.dt.from_np(a.dtype), kind="ExternalInput").ap())
    args.append(nc.dram_tensor("out_0", (BATCH, S, D), F32, kind="ExternalOutput").ap())
    adaln_moe_ffn(nc, *args)
    r = run_bass_kernel_spmd(nc, [arrays], core_ids=[0])
    return r.results[0]["out_0"]
```
